# Optimizing a Trainium2 kernel written in Bass

```python
import numpy as np
import jax
import jax.numpy as jnp

def _softmax(x, axis=-1):
    return jax.nn.softmax(x, axis=axis)

def _gelu(x):
    return jax.nn.gelu(x, approximate=True)

def _silu(x):
    return jax.nn.silu(x)

def _sigmoid(x):
    return jax.nn.sigmoid(x)

def _layernorm(x, axis=-1, eps=1e-05):
    m = jnp.mean(x, axis=axis, keepdims=True)
    v = jnp.var(x, axis=axis, keepdims=True)
    return (x - m) / jnp.sqrt(v + eps)

def _scatter_add(tgt, idx, src, axis=0):
    return tgt.at[idx].add(src)

def _segment_sum(src, seg, n):
    return jax.ops.segment_sum(src, seg, n)
kernel_name = 'mk_gnn_ffn_d1_gnn_r8_d13a0a'

def setup_inputs(seed: int=0):
    np.random.seed(seed)
    _w = jnp.asarray

    def _rec_inputs():
        import jax
        import jax.numpy as jnp
        _gk = jax.random.key(seed)
        x = -8.776e-05 + 1 * jax.random.normal(jax.random.fold_in(_gk, 1), (6250, 256), jnp.float32)
        _s = jax.random.randint(jax.random.fold_in(_gk, 2), (100000,), 0, 6250, jnp.int32)
        _d = jax.random.randint(jax.random.fold_in(_gk, 3), (100000,), 0, 6250, jnp.int32)
        _loop = jnp.arange(6250, dtype=jnp.int32)
        src = jnp.concatenate([_s, _d, _loop])
        dst = jnp.concatenate([_d, _s, _loop])
        _o = jnp.argsort(dst, stable=True)
        src = src[_o]
        dst = dst[_o]
        edge_type_8 = jax.random.randint(jax.random.fold_in(_gk, 12), (206250,), 0, 8, jnp.int32)
        node_type_5 = jax.random.randint(jax.random.fold_in(_gk, 13), (6250,), 0, 5, jnp.int32)
        return (x, src, dst, edge_type_8, node_type_5)
    x, src, dst, edge_type_8, node_type_5 = _rec_inputs()

    def _L0_gnn_setup():
        import jax, jax.numpy as jnp
        import numpy as np
        N = 2500
        E = 80000
        R = 8
        B = 4
        T = 5
        D = 256

        def _rgcn_conv(x, edge_index, edge_type, basis, comp, root, bias):
            n = x.shape[0]
            W = jnp.einsum('rb,bde->rde', comp, basis)
            h = jnp.einsum('nd,rde->nre', x, W)
            src, dst = (edge_index[0], edge_index[1])
            msg = h[src, edge_type]
            seg = dst * R + edge_type
            sums = jax.ops.segment_sum(msg, seg, num_segments=n * R)
            cnt = jax.ops.segment_sum(jnp.ones((msg.shape[0],), msg.dtype), seg, num_segments=n * R)
            mean = sums / jnp.maximum(cnt, 1.0)[:, None]
            agg = mean.reshape(n, R, -1).sum(axis=1)
            return agg + x @ root + bias
        key = jax.random.key(seed)
        ks = jax.random.split(key, 16)
        s = 0.05
        inp = {'x': jax.random.normal(ks[0], (N, D), jnp.float32), 'edge_index': jax.random.randint(ks[1], (2, E), 0, N), 'node_type': jax.random.randint(ks[2], (N,), 0, T), 'edge_type': jax.random.randint(ks[3], (E,), 0, R), 'basis0': jax.random.normal(ks[4], (B, D, D), jnp.float32) * s, 'comp0': jax.random.normal(ks[5], (R, B), jnp.float32) * s, 'root0': jax.random.normal(ks[6], (D, D), jnp.float32) * s, 'bias0': jnp.zeros((D,), jnp.float32), 'basis1': jax.random.normal(ks[7], (B, D, D), jnp.float32) * s, 'comp1': jax.random.normal(ks[8], (R, B), jnp.float32) * s, 'root1': jax.random.normal(ks[9], (D, D), jnp.float32) * s, 'bias1': jnp.zeros((D,), jnp.float32), 'lin_w': jax.random.normal(ks[10], (T, D, D), jnp.float32) * s, 'lin_b': jnp.zeros((T, D), jnp.float32)}
        return inp
    _L0_gnn_all = _L0_gnn_setup()
    _L0_gnn_in = {k: v for k, v in _L0_gnn_all.items() if k in ('basis0', 'comp0', 'root0', 'bias0', 'basis1', 'comp1', 'root1', 'bias1', 'lin_w', 'lin_b')}
    del _L0_gnn_all

    def _L0_ffn_setup():
        import jax, jax.numpy as jnp
        import numpy as np
        E = 8
        K = 2
        D = 256
        H = 512
        DOUT = 256
        EPS = 1e-05
        key = jax.random.key(seed)
        ks = jax.random.split(key, 9)
        s = 0.02
        return {'x': jax.random.normal(ks[0], (4, 1024, D), jnp.float32), 'gamma': 1.0 + 0.05 * jax.random.normal(ks[1], (D,), jnp.float32), 'beta': 0.05 * jax.random.normal(ks[2], (D,), jnp.float32), 'Wr': 0.01 * jax.random.normal(ks[3], (D, E), jnp.float32), 'br': jnp.zeros((E,), jnp.float32), 'W1': s * jax.random.normal(ks[4], (E, D, H), jnp.float32), 'b1': s * jax.random.normal(ks[5], (E, H), jnp.float32), 'W2': s * jax.random.normal(ks[6], (E, H, DOUT), jnp.float32), 'b2': s * jax.random.normal(ks[7], (E, DOUT), jnp.float32)}
    _L0_ffn_all = _L0_ffn_setup()
    _L0_ffn_in = {k: v for k, v in _L0_ffn_all.items() if k in ('gamma', 'beta', 'Wr', 'br', 'W1', 'b1', 'W2', 'b2')}
    del _L0_ffn_all
    return {'x': x, 'src': src, 'dst': dst, 'edge_type_8': edge_type_8, 'node_type_5': node_type_5, 'L0_gnn_basis0': _L0_gnn_in['basis0'], 'L0_gnn_comp0': _L0_gnn_in['comp0'], 'L0_gnn_root0': _L0_gnn_in['root0'], 'L0_gnn_bias0': _L0_gnn_in['bias0'], 'L0_gnn_basis1': _L0_gnn_in['basis1'], 'L0_gnn_comp1': _L0_gnn_in['comp1'], 'L0_gnn_root1': _L0_gnn_in['root1'], 'L0_gnn_bias1': _L0_gnn_in['bias1'], 'L0_gnn_lin_w': _L0_gnn_in['lin_w'], 'L0_gnn_lin_b': _L0_gnn_in['lin_b'], 'L0_ffn_gamma': _L0_ffn_in['gamma'], 'L0_ffn_beta': _L0_ffn_in['beta'], 'L0_ffn_Wr': _L0_ffn_in['Wr'], 'L0_ffn_br': _L0_ffn_in['br'], 'L0_ffn_W1': _L0_ffn_in['W1'], 'L0_ffn_b1': _L0_ffn_in['b1'], 'L0_ffn_W2': _L0_ffn_in['W2'], 'L0_ffn_b2': _L0_ffn_in['b2']}

def reference(x, src, dst, edge_type_8, node_type_5, L0_gnn_basis0, L0_gnn_comp0, L0_gnn_root0, L0_gnn_bias0, L0_gnn_basis1, L0_gnn_comp1, L0_gnn_root1, L0_gnn_bias1, L0_gnn_lin_w, L0_gnn_lin_b, L0_ffn_gamma, L0_ffn_beta, L0_ffn_Wr, L0_ffn_br, L0_ffn_W1, L0_ffn_b1, L0_ffn_W2, L0_ffn_b2):
    import jax
    import jax.numpy as jnp

    def _L0_gnn_ref(x, edge_index, node_type, edge_type, basis0, comp0, root0, bias0, basis1, comp1, root1, bias1, lin_w, lin_b):
        import jax, jax.numpy as jnp
        import numpy as np
        N = 2500
        E = 80000
        R = 8
        B = 4
        T = 5
        D = 256

        def _rgcn_conv(x, edge_index, edge_type, basis, comp, root, bias):
            n = x.shape[0]
            W = jnp.einsum('rb,bde->rde', comp, basis)
            h = jnp.einsum('nd,rde->nre', x, W)
            src, dst = (edge_index[0], edge_index[1])
            msg = h[src, edge_type]
            seg = dst * R + edge_type
            sums = jax.ops.segment_sum(msg, seg, num_segments=n * R)
            cnt = jax.ops.segment_sum(jnp.ones((msg.shape[0],), msg.dtype), seg, num_segments=n * R)
            mean = sums / jnp.maximum(cnt, 1.0)[:, None]
            agg = mean.reshape(n, R, -1).sum(axis=1)
            return agg + x @ root + bias
        h = jax.nn.relu(_rgcn_conv(x, edge_index, edge_type, basis0, comp0, root0, bias0))
        h = jax.nn.relu(_rgcn_conv(h, edge_index, edge_type, basis1, comp1, root1, bias1))
        ht = jnp.einsum('nd,tde->nte', h, lin_w)
        out = jnp.take_along_axis(ht, node_type[:, None, None], axis=1)[:, 0, :]
        return out + lin_b[node_type]

    def _L0_ffn_ref(x, gamma, beta, Wr, br, W1, b1, W2, b2):
        import jax, jax.numpy as jnp
        import numpy as np
        E = 8
        K = 2
        D = 256
        H = 512
        DOUT = 256
        EPS = 1e-05
        mu = jnp.mean(x, axis=-1, keepdims=True)
        var = jnp.mean(jnp.square(x - mu), axis=-1, keepdims=True)
        xn = (x - mu) * jax.lax.rsqrt(var + EPS) * gamma + beta
        logits = jnp.einsum('bsd,de->bse', xn, Wr) + br
        top_vals, top_idx = jax.lax.top_k(logits, K)
        w = jax.nn.softmax(top_vals, axis=-1)
        w_full = jnp.einsum('bsk,bske->bse', w, jax.nn.one_hot(top_idx, E, dtype=w.dtype))
        y = jnp.zeros(x.shape[:-1] + (DOUT,), x.dtype)
        for e in range(E):
            h = jax.nn.gelu(jnp.einsum('bsd,dh->bsh', xn, W1[e]) + b1[e], approximate=False)
            y_e = jnp.einsum('bsh,hd->bsd', h, W2[e]) + b2[e]
            y = y + y_e * w_full[..., e, None]
        return y
    edge_index = jnp.stack([src, dst])
    x = x + _L0_gnn_ref(_layernorm(x, axis=-1), edge_index, node_type_5, edge_type_8, L0_gnn_basis0, L0_gnn_comp0, L0_gnn_root0, L0_gnn_bias0, L0_gnn_basis1, L0_gnn_comp1, L0_gnn_root1, L0_gnn_bias1, L0_gnn_lin_w, L0_gnn_lin_b)
    x = x + _L0_ffn_ref(_layernorm(x, axis=-1)[None], L0_ffn_gamma, L0_ffn_beta, L0_ffn_Wr, L0_ffn_br, L0_ffn_W1, L0_ffn_b1, L0_ffn_W2, L0_ffn_b2)[0]
    return x

_drawn_inputs = setup_inputs


def setup_inputs(seed=0):
    import zlib

    import numpy as np

    out = dict(_drawn_inputs(seed))
    spreads = {'L0_gnn_bias0': (0.0, 0.1),
     'L0_gnn_bias1': (0.0, 0.1),
     'L0_gnn_lin_b': (0.0, 0.1),
     'L0_ffn_br': (0.0, 0.1)}
    factors = {'L0_ffn_gamma': 6.276, 'L0_ffn_beta': 5.211, 'L0_ffn_b1': 8.0, 'L0_ffn_b2': 4.403}
    for name, (base, spread) in spreads.items():
        noise = np.random.default_rng([zlib.crc32(name.encode()), seed]).standard_normal(out[name].shape)
        drawn = base * np.exp(spread * noise) if base else spread * noise
        out[name] = jnp.asarray(drawn.astype(out[name].dtype))
    for name, factor in factors.items():
        out[name] = (out[name] * factor).astype(out[name].dtype)
    return out
```

```python
from contextlib import ExitStack
import math

import concourse.bass as bass
from concourse import mybir

ALU = mybir.AluOpType
ACT = mybir.ActivationFunctionType
AX = mybir.AxisListType
F32 = mybir.dt.float32
BF16 = mybir.dt.bfloat16
I32 = mybir.dt.int32
U32 = mybir.dt.uint32

P = 128
N, D, E, R, NBASIS, TYPES = 6250, 256, 206250, 8, 4, 5
EXPERTS, HID = 8, 512
EPS = 1e-5
HALVES = D // P
HCH = HID // P
BD = 64
SLOTS = BD * R
BLOCKS = -(-N // BD)
PAIRS = -(-N // P)
NPAD = PAIRS * P
LAST = N - (PAIRS - 1) * P
MEAN = E / N
START = 1
RUN = 3
TILES = 18
CAP = TILES * P
EROWS, ECOLS = 125, E // 125
EWINDOWS = E // CAP + 2
PADLEN, PADROWS = EWINDOWS * CAP - E, 6
PADKEY = float(BLOCKS * SLOTS)
GROUP = 7
GROUPS = PAIRS // GROUP
PARTS = 3
MROWS = (BLOCKS + 1) * SLOTS
SPARE = BLOCKS * SLOTS + P
STEPS = -(-E // P)
QUADS = SLOTS // P
MCOLS = D + 1


def tile_windows():
    out = []
    for k in range(TILES):
        a, b = P * k / MEAN, (P * k + P - 1) / MEAN
        spread = 4.5 * math.sqrt(MEAN - 1) / MEAN
        out.append((max(0, math.floor(a - spread * math.sqrt(a) - 0.5)),
                    min(BD, math.ceil(b + spread * math.sqrt(b) + 0.5) + 1)))
    return out


WIN = tile_windows()
HOT_AT = [R * sum(hi - lo for lo, hi in WIN[:k]) for k in range(TILES + 1)]
HOT_MAX = R * max(hi - lo for lo, hi in WIN)


class Chain:

    def __init__(self, eng, sem):
        self.eng, self.sem, self.base, self.n = eng, sem, 0, 0

    def begin(self, base):
        self.base, self.n = base, 0

    def link(self, ins):
        self.n += 1
        ins.then_inc(self.sem, 1)
        self.eng.wait_ge(self.sem, self.base + self.n)


def build(nc, x, src, dst, etype, ntype, basis0, comp0, root0, bias0, basis1, comp1, root1, bias1,
          lin_w, lin_b, gamma, beta, Wr, br, W1, b1, W2, b2, out):
    with ExitStack() as ctx:
        def sb(name, shape, dt):
            return ctx.enter_context(nc.sbuf_tensor(name, shape, dt))

        def sem(name):
            return ctx.enter_context(nc.semaphore(name))

        def dram(name, shape, dt):
            return nc.dram_tensor(name, shape, dt, kind="Internal").ap()

        key_d = dram("key_d", (EWINDOWS * CAP,), F32)
        src_d = dram("src_d", (EWINDOWS * CAP,), F32)
        table = [dram("table0", (NPAD, PARTS * D), BF16), dram("table1", (NPAD, PARTS * D), BF16)]
        idx_d = dram("idx_d", (P, BLOCKS, TILES), I32)
        rel_d = dram("rel_d", (P, BLOCKS, TILES), F32)
        inv_d = dram("inv_d", (BLOCKS, SLOTS), F32)

        sums_d = dram("sums_d", (MROWS, MCOLS), F32)

        featT = sb("featT", [P, HALVES, NPAD], F32)
        slot = sb("slot", [P, TILES, PARTS * D], BF16)
        wrel = sb("wrel", [P, R, HALVES, D], F32)
        scaled = sb("scaled", [P, HALVES, R, P], F32)
        basis = scaled[:, :, :, :].rearrange("p a r n -> p (a r n)").rearrange(
            "p (b k e) -> p b k e", b=NBASIS, k=HALVES)
        ffn_w = sb("ffn_w", [P, HALVES * EXPERTS * HID + EXPERTS * HCH * D], F32)
        w1_sb = ffn_w[:, 0:HALVES * EXPERTS * HID].rearrange("p (e k h) -> p e k h", e=EXPERTS, k=HALVES)
        w2_sb = ffn_w[:, HALVES * EXPERTS * HID:].rearrange("p (e c d) -> p e c d", e=EXPERTS, c=HCH)
        linw_sb = sb("linw_sb", [P, TYPES, HALVES, D], F32)
        root_sb = sb("root_sb", [P, HALVES, D], F32)
        wr_sb = sb("wr_sb", [P, HALVES, EXPERTS], F32)
        small = sb("small", [P, 96], F32)
        bias_sb = [small[:, 0:2], small[:, 2:4]]
        gamma_sb, beta_sb = small[:, 4:6], small[:, 6:8]
        b1_sb = small[:, 8:40]
        comp_sb = [small[:, 40:72], sb("comp1_sb", [P, R * NBASIS], F32)[:, :]]
        linb_sb = sb("linb_sb", [TYPES, D], F32)
        b2_sb = sb("b2_sb", [EXPERTS, D], F32)
        br_sb = sb("br_sb", [1, EXPERTS], F32)
        ident = sb("ident", [P, P], F32)
        ones_b = sb("ones_b", [P, P], BF16)
        ones_f = sb("ones_f", [P, P], F32)
        iota_b = sb("iota_b", [P, HOT_MAX], BF16)
        iota8 = sb("iota8", [P, EXPERTS], F32)
        pid = sb("pid", [P, 1], F32)
        hot = sb("hot", [P, 2, HOT_AT[TILES]], BF16)
        idx = sb("idx", [P, 2, TILES], I32)
        rel = sb("rel", [P, 2, TILES], F32)
        inv = sb("inv", [P, 2, SLOTS], F32)
        hcur = sb("hcur", [P, HALVES, P], F32)
        parts = sb("parts", [P, PARTS, D], BF16)
        rest = sb("rest", [P, D], F32)
        xcur = sb("xcur", [P, D], F32)
        ntcol = sb("ntcol", [P, 1], I32)
        ntrow = sb("ntrow", [TYPES, P], I32)
        tmask = sb("tmask", [P, TYPES], F32)
        tmaskT = sb("tmaskT", [TYPES, P], F32)
        x1 = sb("x1", [P, D], F32)
        zn = sb("zn", [P, D], F32)
        stats = sb("stats", [P, 6], F32)
        mv = sb("mv", [P, 2], F32)
        rstd = sb("rstd", [P, 1], F32)
        idle = sb("idle", [P, 1], F32)
        std = sb("std", [P, 1], F32)
        xnT = sb("xnT", [P, HALVES, P], F32)
        lg = sb("lg", [P, EXPERTS], F32)
        top = sb("top", [P, 8], F32)
        topi = sb("topi", [P, 8], U32)
        topf = sb("topf", [P, 2], F32)
        soft = sb("soft", [P, 4], F32)
        wfull = sb("wfull", [P, 2, EXPERTS], F32)
        wfT = sb("wfT", [EXPERTS, P], F32)
        act = sb("act", [P, 2, HCH, P], F32)
        o = sb("o", [P, D], F32)

        def carve(t, at, n):
            return t[:, at:at + n]
        GW = GROUP * D
        xg = [carve(ffn_w, i * GW, GW).rearrange("p (t d) -> p t d", t=GROUP) for i in range(2)]
        xn = [carve(ffn_w, (2 + i) * GW, GW).rearrange("p (t d) -> p t d", t=GROUP) for i in range(2)]
        grest = carve(ffn_w, 4 * GW, GW).rearrange("p (t d) -> p t d", t=GROUP)
        gparts = [carve(ffn_w, 5 * GW + i * PARTS * GW // 2, PARTS * GW // 2).bitcast(BF16).rearrange(
            "p (t q d) -> p t q d", t=GROUP, q=PARTS) for i in range(2)]
        gvar = sb("gvar", [P, GROUP], F32)
        eps_col = sb("eps_col", [P, 1], F32)
        gstats = sb("gstats", [P, GROUP, 6], F32)
        gmv = sb("gmv", [P, GROUP, 2], F32)
        grstd = sb("grstd", [P, 2, GROUP], F32)
        gshift = sb("gshift", [P, 2, GROUP], F32)
        early = slot[:, :, :].rearrange("p t d -> p (t d)").bitcast(F32)
        raw = early[0:EROWS, 0:3 * ECOLS].bitcast(I32).rearrange("p (a c) -> p a c", a=3)
        win = early[0:BLOCKS, 0:2 * CAP].rearrange("p (a c) -> p a c", a=2)
        late = wrel[:, :, :, :].rearrange("p r k d -> p (r k d)")
        edge_f = late[0:EROWS, 0:2 * ECOLS].rearrange("p (a c) -> p a c", a=2)
        rows = linw_sb[:, :, :, :].rearrange("p t k d -> p (t k d)")[0:BLOCKS, 0:ECOLS]
        idx_all = carve(ffn_w, 5 * GW + PARTS * GW, BLOCKS * TILES).bitcast(I32).rearrange(
            "p (b t) -> p b t", t=TILES)
        rel_all = hot[:, :, :].rearrange("p a c -> p (a c)").bitcast(F32)[:, 0:BLOCKS * TILES].rearrange(
            "p (b t) -> p b t", t=TILES)
        padt = [inv[0:PADROWS, :, :].rearrange("p a c -> p (a c)")[:, 0:PADLEN // PADROWS],
                act[0:PADROWS, :, :, :].rearrange("p a c n -> p (a c n)")[:, 0:PADLEN // PADROWS]]
        limit_col = sb("limit_col", [P, 1], F32)
        limit_row = x1[:, 0:BLOCKS]
        before = x1[:, P:P + BLOCKS]
        found = sb("found", [P, 4], F32)
        row_i = sb("row_i", [P, 1], I32)
        start_i = sb("start_i", [P, 1], I32)

        MW = QUADS * MCOLS
        sums_sb = [carve(early, i * MW, MW).rearrange("p (q c) -> p q c", q=QUADS) for i in range(2)]
        zeros = carve(early, 2 * MW, MW)
        g_rows = carve(early, 3 * MW, PARTS * D // 2).bitcast(BF16)
        g_sum = carve(early, 3 * MW + 384, MCOLS)
        same = carve(early, 3 * MW + 648, P // 2).bitcast(BF16)
        below = carve(early, 3 * MW + 712, P)
        before_me = carve(early, 3 * MW + 840, P)
        g_key = carve(early, 3 * MW + 968, 1)
        g_srcf = carve(early, 3 * MW + 969, 1)
        g_src = carve(early, 3 * MW + 970, 1).bitcast(I32)
        g_dest = carve(early, 3 * MW + 971, 1).bitcast(I32)
        g_tmp = carve(early, 3 * MW + 972, 3)
        spare_row = carve(early, 3 * MW + 975, 1)
        in_window = xg[0].rearrange("p t d -> p (t d)")[:, 0:BLOCKS * TILES].rearrange("p (b t) -> p b t", t=TILES)
        general_i = sb("general_i", [1, 1], I32)

        bank = [ctx.enter_context(nc.psum_tensor(f"bank{i}", [P, 512], F32)) for i in range(8)]
        S = bank[0:2]
        T, T2, C = bank[2], bank[3], bank[4]
        HP = bank[4:6]
        YP = bank[6:8]

        raw_in = [sem(f"raw_in{i}") for i in range(3)]
        s_const = sem("s_const")
        weights_in = sem("weights_in")
        basis_in = [sem(f"basis_in{i}") for i in range(2)]
        ffn_in = sem("ffn_in")
        edges_f = sem("edges_f")
        edges_out = sem("edges_out")
        s_before = sem("s_before")
        s_count = sem("s_count")
        row_ready = sem("row_ready")
        rows_in = sem("rows_in")
        start_ready = sem("start_ready")
        win_in = sem("win_in")
        win_rel = sem("win_rel")
        win_T = sem("win_T")
        win_copied = sem("win_copied")
        tables_ready = sem("tables_ready")
        same_ready = sem("same_ready")
        s_general = sem("s_general")
        tables_out = sem("tables_out")
        pool_waited = sem("pool_waited")
        sp_waited = sem("sp_waited")
        s_dve = sem("s_dve")
        s_wrel = sem("s_wrel")
        xg_in = [sem(f"xg_in{i}") for i in range(2)]
        g_stat = sem("g_stat")
        g_norm = sem("g_norm")
        g_var = sem("g_var")
        g_std = sem("g_std")
        ln_var = sem("ln_var")
        ln_std = sem("ln_std")
        margin_done = sem("margin_done")
        tanh_done = sem("tanh_done")
        g_hi = sem("g_hi")
        g_rest = sem("g_rest")
        g_mid = sem("g_mid")
        g_lo = sem("g_lo")
        g_T = sem("g_T")
        g_Tc = sem("g_Tc")
        g_out = [sem(f"g_out{i}") for i in range(2)]
        idx_in = [sem(f"idx_in{i}") for i in range(2)]
        gathered = [sem(f"gathered{k}") for k in range(TILES)]
        used = {k: sem(f"used{k}") for k in range(RUN - 1, TILES, RUN)}
        hot_ready = sem("hot_ready")
        sc_ready = sem("sc_ready")
        tr_done = sem("tr_done")
        relu_done = sem("relu_done")
        hT_done = sem("hT_done")
        feat_saved = sem("feat_saved")
        hi_done = sem("hi_done")
        rest_done = sem("rest_done")
        mid_done = sem("mid_done")
        lo_done = sem("lo_done")
        parts_out = sem("parts_out")
        inv_out = sem("inv_out")
        inv_in = [sem(f"inv_in{i}") for i in range(2)]
        node_in = sem("node_in")
        mask_done = sem("mask_done")
        lin_ps = sem("lin_ps")
        lin_acc = sem("lin_acc")
        zn_done = sem("zn_done")
        znT_done = sem("znT_done")
        xnT_done = sem("xnT_done")
        lg_done = sem("lg_done")
        lg_read = sem("lg_read")
        wf_done = sem("wf_done")
        wfT_ps = sem("wfT_ps")
        wfT_done = sem("wfT_done")
        h_ps = sem("h_ps")
        h_act = sem("h_act")
        y_ps = sem("y_ps")
        y_acc = sem("y_acc")
        b2_ps = sem("b2_ps")
        o_done = sem("o_done")
        out_done = sem("out_done")
        N_WEIGHTS = 12
        matched = sem("matched")
        matched_sum = sem("matched_sum")
        general_known = sem("general_known")
        zeros_made = sem("zeros_made")
        below_made = sem("below_made")
        sums_cleared = sem("sums_cleared")
        edge_in = sem("edge_in")
        edge_idx = sem("edge_idx")
        key_row = sem("key_row")
        dest_ready = sem("dest_ready")
        edge_rows = sem("edge_rows")
        edge_sum = sem("edge_sum")
        edge_sum_out = sem("edge_sum_out")
        added = sem("added")
        sums_in = [sem(f"sums_in{i}") for i in range(2)]

        def summed(eng, G, h, back=0):
            eng.wait_ge(used[TILES - 1], G * 2 + (START + h + 1 - back))

        def is_general(eng):
            eng.wait_ge(general_known, 1)
            return eng.value_load(general_i[0:1, 0:1], min_val=0, max_val=1)

        block = ctx.enter_context(nc.Block())

        x_g = x[0:(GROUPS - 1) * GROUP * P, :].rearrange("(g t p) d -> g p t d", t=GROUP, p=P)
        tab_g = table[0].rearrange("(g t p) d -> g p t d", t=GROUP, p=P)
        tab_p = table[1].rearrange("(g p) d -> g p d", p=P)
        inv_p = inv_d.rearrange("(g a) s -> g a s", a=2)

        @block.sync
        def _(sp):
            for q in (relu_done, rest_done, o_done, mid_done, lo_done, znT_done, lin_acc, *used.values()):
                sp.sem_inc(q, START)
            for i, a in enumerate((dst, etype, src)):
                sp.dma_start(raw[:, i, :], a.rearrange("(p c) -> p c", p=EROWS)).then_inc(raw_in[i], 16)

            def load_group(i, g):
                if not isinstance(g, int) or g >= 2:
                    sp.wait_ge(g_norm, g - 1)
                if isinstance(g, int) and g == GROUPS - 1:
                    base = g * GROUP * P
                    sp.dma_start(xg[i][:, 0:GROUP - 1, :], x[base:base + (GROUP - 1) * P, :].rearrange(
                        "(t p) d -> p t d", p=P)).then_inc(xg_in[i], 16)
                    sp.dma_start(xg[i][0:LAST, GROUP - 1, :], x[N - LAST:N, :]).then_inc(xg_in[i], 16)
                else:
                    src_ap = x_g[g] if isinstance(g, int) else x_g[bass.ds(g, 1), :, :, :].rearrange(
                        "a p t d -> (a p) t d")
                    sp.dma_start(xg[i], src_ap).then_inc(xg_in[i], 16)

            load_group(0, 0)
            load_group(1, 1)
            sp.wait_ge(edges_f, 2)
            for i, a in enumerate((key_d, src_d)):
                sp.dma_start(a[0:E].rearrange("(p c) -> p c", p=EROWS), edge_f[:, i, :]).then_inc(edges_out, 16)
            sp.wait_ge(s_const, 1)
            for i, a in enumerate((key_d, src_d)):
                sp.dma_start(a[E:EWINDOWS * CAP].rearrange("(p c) -> p c", p=PADROWS), padt[i]).then_inc(edges_out, 16)
            sp.dma_start(root_sb[:, :, :], root0.rearrange("(k p) e -> p k e", p=P)).then_inc(weights_in, 16)
            for v, a in ((bias_sb[0], bias0), (bias_sb[1], bias1), (gamma_sb, gamma), (beta_sb, beta)):
                with nc.allow_non_contiguous_dma(reason="256 values once"):
                    sp.dma_start(v, a.rearrange("(k p) -> p k", p=P)).then_inc(weights_in, 16)
            for v, a in zip(comp_sb, (comp0, comp1)):
                sp.dma_start(v, a.rearrange("r b -> (r b)").partition_broadcast(P)).then_inc(weights_in, 16)
            with nc.allow_non_contiguous_dma(reason="4096 values once"):
                sp.dma_start(b1_sb.rearrange("p (e c) -> p e c", e=EXPERTS),
                             b1.rearrange("e (c p) -> p e c", p=P)).then_inc(weights_in, 16)
            sp.dma_start(linb_sb[:, :], lin_b).then_inc(weights_in, 16)
            sp.dma_start(b2_sb[:, :], b2).then_inc(weights_in, 16)
            sp.dma_start(br_sb[:, :], br.rearrange("(a e) -> a e", a=1)).then_inc(weights_in, 16)
            sp.dma_start(wr_sb[:, :, :], Wr.rearrange("(k p) e -> p k e", p=P)).then_inc(weights_in, 16)
            sp.dma_start(basis, basis0.rearrange("b (k p) e -> p b k e", p=P)).then_inc(basis_in[0], 16)

            def store_group(i, g):
                sp.wait_ge(g_hi, g + 1)
                sp.wait_ge(g_mid, g + 1)
                sp.wait_ge(g_lo, g + 1)
                dst_ap = tab_g[g] if isinstance(g, int) else tab_g[bass.ds(g, 1), :, :, :].rearrange(
                    "a p t d -> (a p) t d")
                sp.dma_start(dst_ap, gparts[i].rearrange("p t q d -> p t (q d)")).then_inc(g_out[i], 16)

            with sp.Fori(0, (GROUPS - 1) // 2 - 1) as g2:
                for i in range(2):
                    store_group(i, g2 * 2 + i)
                    load_group(i, g2 * 2 + i + 2)
            store_group(0, GROUPS - 3)
            load_group(0, GROUPS - 1)
            store_group(1, GROUPS - 2)
            store_group(0, GROUPS - 1)
            sp.wait_ge(tables_ready, 1)
            sp.dma_start(idx_d, idx_all[:, :, :]).then_inc(tables_out, 16)
            sp.dma_start(rel_d, rel_all).then_inc(tables_out, 16)
            sp.wait_ge(tables_out, 32)

            general = is_general(sp)

            def plain():
                sp.sem_inc(sp_waited, 1)

            def load_edges(h, G, p):
                summed(sp, G, h, back=2)
                plain()
                b = p * 2 + h
                with sp.If(general):
                    sp.dma_start(sums_sb[h], sums_d[bass.ds(b * SLOTS, SLOTS), :].rearrange(
                        "(q p) c -> p q c", p=P)).then_inc(sums_in[h], 16)
                with sp.Else():
                    load_tables(h, b)

            def general_sums(layer):
                sp.wait_ge(zeros_made, layer + 1)
                with sp.Fori(layer * (BLOCKS + 1), (layer + 1) * (BLOCKS + 1)) as b:
                    at = b - layer * (BLOCKS + 1)
                    sp.dma_start(sums_d[bass.ds(at * SLOTS, SLOTS), :].rearrange("(p q) c -> p (q c)", p=P),
                                 zeros).then_inc(sums_cleared, 16)
                    sp.wait_ge(sums_cleared, b * 16 + 16)
                    plain()
                with sp.Fori(0, STEPS) as i:
                    for v, a in ((g_key, key_d), (g_srcf, src_d)):
                        sp.dma_start(v, a[bass.ds(i * P, P)].rearrange("(p a) -> p a", a=1)).then_inc(edge_in, 16)
                    sp.wait_ge(added, i * 16 + (layer * STEPS * 16 + 16))
                    plain()

            def load_tables(h, b):
                cut = bass.ds(b, 1)
                sp.dma_start(idx[:, h, :], idx_d[:, cut, :].rearrange("p a t -> p (a t)")).then_inc(idx_in[h], 16)
                sp.dma_start(rel[:, h, :], rel_d[:, cut, :].rearrange("p a t -> p (a t)")).then_inc(idx_in[h], 16)

            def store_inv(p):
                sp.wait_ge(sc_ready, p * 2 + 2)
                sp.dma_start(inv_p[bass.ds(p, 1), :, :], inv[0:1, :, :]).then_inc(inv_out, 16)

            with sp.If(general):
                for i in range(2):
                    sp.wait_ge(g_out[i], 16 * (4 - i))
                general_sums(0)
            for h in range(2):
                load_edges(h, 0, 0)
            with sp.Fori(1, PAIRS) as p:
                for h in range(2):
                    load_edges(h, p, p)
                store_inv(p - 1)
            store_inv(PAIRS - 1)

            for i in range(2):
                sp.wait_ge(g_out[i], 16 * (4 - i))
            sp.wait_ge(g_Tc, GROUPS)
            sp.dma_start(w1_sb.rearrange("p e k h -> p (e k) h"),
                         W1.rearrange("e (k p) h -> p (e k) h", p=P)).then_inc(ffn_in, 16)
            sp.dma_start(w2_sb.rearrange("p e c d -> p (e c) d"),
                         W2.rearrange("e (c p) d -> p (e c) d", p=P)).then_inc(ffn_in, 16)
            sp.dma_start(linw_sb[:, :, :, :].rearrange("p t k d -> p (t k) d"),
                         lin_w.rearrange("t (k p) d -> p (t k) d", p=P)).then_inc(ffn_in, 16)

            sp.wait_ge(tr_done, PAIRS)
            sp.dma_start(root_sb[:, :, :], root1.rearrange("(k p) e -> p k e", p=P)).then_inc(basis_in[1], 16)
            sp.dma_start(basis, basis1.rearrange("b (k p) e -> p b k e", p=P)).then_inc(basis_in[1], 16)
            sp.wait_ge(inv_out, 16 * PAIRS)

            def load_inv(h, G, p):
                sp.wait_ge(sc_ready, (G * 2 + h) - 1)
                sp.dma_start(inv[:, h, :], inv_p[bass.ds(p, 1), h, :].rearrange(
                    "a s -> (a s)").partition_broadcast(P)).then_inc(inv_in[h], 16)

            def load_nodes(p, n=P):
                sp.wait_ge(lin_acc, START + 6 * p)
                at = bass.ds(p * P, n)
                sp.dma_start(xcur[0:n, :], x[at, :]).then_inc(node_in, 16)
                sp.dma_start(ntcol[0:n, :], ntype[at].rearrange("(p a) -> p a", a=1)).then_inc(node_in, 16)
                sp.dma_start(ntrow[:, 0:n], ntype[at].partition_broadcast(TYPES)).then_inc(node_in, 16)

            with sp.If(general):
                sp.wait_ge(parts_out, 16 * PAIRS)
                general_sums(1)
            for h in range(2):
                load_edges(h, PAIRS, 0)
                load_inv(h, PAIRS, 0)
            with sp.Fori(1, PAIRS) as p:
                for h in range(2):
                    load_edges(h, p + PAIRS, p)
                    load_inv(h, p + PAIRS, p)
                load_nodes(p - 1)
            load_nodes(PAIRS - 1, LAST)
            sp.wait_ge(out_done, 16 * PAIRS)

        @block.gpsimd
        def _(gp):
            def plain():
                gp.sem_inc(pool_waited, 1)

            gp.memset(padt[0], PADKEY)
            gp.memset(padt[1], 0.0).then_inc(s_const, 1)
            gp.memset(ones_f[:, :], 1.0)
            gp.memset(ones_b[:, :], 1.0)
            gp.memset(eps_col[:, :], EPS)
            gp.iota(limit_col[:, :], [[0, 1]], base=0, channel_multiplier=SLOTS,
                    allow_small_or_imprecise_dtypes=True)
            gp.iota(limit_row[:, :], [[SLOTS, BLOCKS]], base=0, channel_multiplier=0,
                    allow_small_or_imprecise_dtypes=True)
            gp.iota(iota_b[:, :], [[1, HOT_MAX]], base=0, channel_multiplier=0,
                    allow_small_or_imprecise_dtypes=True)
            gp.iota(iota8[:, :], [[1, EXPERTS]], base=0, channel_multiplier=0,
                    allow_small_or_imprecise_dtypes=True)
            gp.iota(pid[:, :], [[0, 1]], base=0, channel_multiplier=1, allow_small_or_imprecise_dtypes=True)
            gp.memset(ident[:, :], 0.0).then_inc(s_const, 1)
            gp.wait_ge(s_const, 2)
            gp.affine_select(out=ident[:, :], in_=ident[:, :], compare_op=ALU.not_equal, fill=1.0, base=0,
                             pattern=[[-1, P]], channel_multiplier=1).then_inc(s_const, 1)

            gp.wait_ge(row_ready, 1)
            gp.wait_ge(edges_out, 64)
            gp.indirect_dma_start(out=rows, out_offset=None, in_=key_d[0:E].rearrange("(p c) -> p c", c=ECOLS),
                                  in_offset=bass.IndirectOffsetOnAxis(ap=row_i[0:BLOCKS, 0:1], axis=0)).then_inc(rows_in, 16)
            gp.wait_ge(start_ready, 1)
            for i, a in enumerate((key_d, src_d)):
                gp.indirect_dma_start(out=win[:, i, :], out_offset=None,
                                      in_=a.rearrange("(p c) -> p c", c=CAP),
                                      in_offset=bass.IndirectOffsetOnAxis(ap=start_i[0:BLOCKS, 0:1], axis=1)).then_inc(win_in, 16)

            def mid(i, g):
                gp.wait_ge(g_rest, g + 1)
                gp.wait_ge(g_out[i], 16 * ((g - i) // 2) if isinstance(g, int) else 8 * (g - i))
                gp.tensor_copy(gparts[i][:, :, 1, :], grest).then_inc(g_mid, 1)

            mid(0, 0)
            mid(1, 1)
            with gp.Fori(1, (GROUPS - 1) // 2) as g2:
                for i in range(2):
                    gp.wait_ge(g_rest, g2 * 2 + i + 1)
                    gp.wait_ge(g_out[i], g2 * 16)
                    plain()
                    gp.tensor_copy(gparts[i][:, :, 1, :], grest).then_inc(g_mid, 1)
            mid(0, GROUPS - 1)

            def gathers(layer, G):
                blocks = [gp.snap(G * 2 + (START + h)) for h in range(2)]
                for h in range(2):
                    n = blocks[h]
                    gp.wait_ge(idx_in[h], G * 32 + 32)
                    for k in range(TILES):
                        if k % RUN == 0:
                            gp.wait_ge(used[k + RUN - 1], n)
                            plain()
                        gp.indirect_dma_start(out=slot[:, k, :], out_offset=None, in_=table[layer],
                                              in_offset=bass.IndirectOffsetOnAxis(ap=idx[:, h, k:k + 1], axis=0)).then_inc(gathered[k], 16)

            def general_sums(layer):
                gp.memset(zeros, 0.0)
                gp.memset(below, 0.0).then_inc(zeros_made, 1)
                gp.wait_ge(zeros_made, layer + 1)
                gp.iota(spare_row, [[0, 1]], base=SPARE, channel_multiplier=1,
                        allow_small_or_imprecise_dtypes=True)
                gp.affine_select(out=below, in_=below, compare_op=ALU.is_ge, fill=1.0, base=0,
                                 pattern=[[1, P]], channel_multiplier=-1).then_inc(below_made, 1)
                with gp.Fori(0, STEPS) as i:
                    n = i + layer * STEPS
                    gp.wait_ge(edge_idx, n + 1)
                    plain()
                    gp.indirect_dma_start(out=g_rows, out_offset=None, in_=table[layer],
                                          in_offset=bass.IndirectOffsetOnAxis(ap=g_src, axis=0)).then_inc(edge_rows, 16)
                    gp.wait_ge(dest_ready, n + 1)
                    plain()
                    gp.wait_ge(edge_sum_out, n + 1)
                    plain()
                    gp.indirect_dma_start(out=sums_d, out_offset=bass.IndirectOffsetOnAxis(ap=g_dest, axis=0),
                                          in_=g_sum, in_offset=None, compute_op=ALU.add).then_inc(added, 16)
                    gp.wait_ge(added, n * 16 + 16)
                    plain()

            for i in range(2):
                gp.wait_ge(g_out[i], 16 * (4 - i))
            general = is_general(gp)
            with gp.If(general):
                general_sums(0)
                gp.wait_ge(parts_out, 16 * PAIRS)
                general_sums(1)
            with gp.Else():
                with gp.Fori(0, PAIRS) as p:
                    gathers(0, p)
                gp.wait_ge(parts_out, 16 * PAIRS)
                with gp.Fori(PAIRS, 2 * PAIRS) as p:
                    gathers(1, p)

        @block.scalar
        def _(act_):
            sc = nc.scalar

            def norm_group(i, g):
                act_.wait_ge(g_var, g + 1)
                sc.activation(gvar[:, :], gvar[:, :], ACT.Sqrt, bias=eps_col[:, :]).then_inc(g_std, 1)
                act_.wait_ge(g_stat, g + 1)
                if not isinstance(g, int) or g >= 2:
                    act_.wait_ge(g_Tc, g - 1)
                    act_.wait_ge(g_rest, g - 1)
                for t in range(GROUP):
                    last = sc.activation(xn[i][:, t, :], xg[i][:, t, :], ACT.Identity,
                                         bias=gshift[:, i, t:t + 1], scale=grstd[:, i, t:t + 1])
                last.then_inc(g_norm, 1)
                act_.wait_ge(g_norm, g + 1)
                if not isinstance(g, int) or g >= 2:
                    act_.wait_ge(g_out[i], 8 * (g - i))
                sc.activation(gparts[i][:, :, 0, :], xn[i], ACT.Copy).then_inc(g_hi, 1)
                for j in range(4):
                    n = min(4, 2 * GROUP - 4 * j) // 2
                    act_.wait_ge(g_T, g * 4 + j + 1)
                    node = g * (GROUP * P) + j * 2 * P
                    for k in range(HALVES):
                        last = sc.activation(featT[:, k, bass.ds(node, n * P)],
                                             bank[j][:, k * n * P:(k + 1) * n * P], ACT.Copy)
                last.then_inc(g_Tc, 1)

            norm_group(0, 0)
            norm_group(1, 1)
            with act_.Fori(1, (GROUPS - 1) // 2) as g2:
                for i in range(2):
                    norm_group(i, g2 * 2 + i)
            norm_group(0, GROUPS - 1)

            act_.wait_ge(weights_in, 16 * N_WEIGHTS)

            def relu(layer, G, p):
                act_.wait_ge(tr_done, G + 1)
                if layer == 0:
                    act_.wait_ge(hT_done, p)
                    act_.wait_ge(feat_saved, p)
                for k in range(HALVES):
                    last = sc.activation(hcur[:, k, :], T[:, k * P:(k + 1) * P], ACT.Relu,
                                         bias=bias_sb[layer][:, k:k + 1])
                last.then_inc(relu_done, 1)

            def publish(p):
                act_.wait_ge(hT_done, p + 1)
                act_.wait_ge(parts_out, p * 16)
                sc.activation(parts[:, 0, :], T2[:, 0:D], ACT.Copy).then_inc(hi_done, 1)
                act_.wait_ge(rest_done, START + p + 1)
                sc.activation(parts[:, 1, :], rest[:, :], ACT.Copy).then_inc(mid_done, 1)
                act_.wait_ge(lo_done, START + p + 1)
                act_.wait_ge(mid_done, START + p + 1)
                act_.dma_start(tab_p[bass.ds(p, 1), :, :].rearrange("a p d -> (a p) d"),
                               parts[:, :, :].rearrange("p q d -> p (q d)")).then_inc(parts_out, 16)

            relu(0, 0, 0)
            publish(0)
            with act_.Fori(1, PAIRS) as p:
                relu(0, p, p)
                publish(p)

            def dense(p, n=P):
                act_.wait_ge(out_done, p * 16)
                relu(1, p + PAIRS, p)
                for i in range(2):
                    act_.wait_ge(ln_var, p * 2 + i + 1)
                    sc.activation(std[:, :], mv[:, 1:2], ACT.Sqrt, bias=eps_col[:, :]).then_inc(ln_std, 1)
                act_.wait_ge(znT_done, START + p + 1)
                for k in range(HALVES):
                    last = sc.activation(xnT[:, k, :], T2[:, k * P:(k + 1) * P], ACT.Identity,
                                         bias=beta_sb[:, k:k + 1], scale=gamma_sb[:, k:k + 1])
                last.then_inc(xnT_done, 1)
                act_.wait_ge(margin_done, p + 1)
                sc.activation(soft[:, 1:2], soft[:, 0:1], ACT.Tanh, scale=0.5).then_inc(tanh_done, 1)
                for e in range(EXPERTS):
                    act_.wait_ge(h_ps, p * EXPERTS + e + 1)
                    if e >= 2:
                        act_.wait_ge(y_ps, p * EXPERTS + e - 1)
                    for c in range(HCH):
                        last = sc.activation(act[:, e % 2, c, :], HP[e % 2][:, c * P:(c + 1) * P], ACT.Gelu,
                                             bias=b1_sb[:, e * HCH + c:e * HCH + c + 1])
                    last.then_inc(h_act, 1)
                    if e == 4:
                        act_.wait_ge(wfT_ps, p + 1)
                        sc.activation(wfT[:, :], T2[0:EXPERTS, 256:256 + P], ACT.Copy).then_inc(wfT_done, 1)
                act_.wait_ge(o_done, START + p + 1)
                act_.dma_start(out[bass.ds(p * P, n), :], o[0:n, :]).then_inc(out_done, 16)

            dense(0)
            with act_.Fori(1, PAIRS - 1) as p:
                dense(p)
            dense(PAIRS - 1, LAST)
            act_.wait_ge(out_done, 16 * PAIRS)

        @block.vector
        def _(dve):
            v = nc.vector
            ch = Chain(dve, s_dve)
            chg = Chain(dve, s_general)

            def plain():
                v.memset(idle[:, :], 0.0)

            dve.wait_ge(s_const, 3)
            for i in range(3):
                dve.wait_ge(raw_in[i], 16)
            v.scalar_tensor_tensor(out=edge_f[:, 0, :], in0=raw[:, 0, :], scalar=float(R), in1=raw[:, 1, :],
                                   op0=ALU.mult, op1=ALU.add).then_inc(edges_f, 1)
            v.tensor_copy(edge_f[:, 1, :], raw[:, 2, :]).then_inc(edges_f, 1)
            dve.wait_ge(edges_f, 2)
            v.tensor_scalar(before[0:EROWS, :], limit_row[0:EROWS, :], edge_f[:, 0, 0:1], None,
                            ALU.is_gt).then_inc(s_before, 1)
            dve.wait_ge(s_count, 1)
            B = slice(0, BLOCKS)
            ch.link(v.tensor_scalar(found[B, 0:1], T[B, 0:1], -1.0, 0.0, ALU.add, ALU.max))
            v.tensor_copy(row_i[B, :], found[B, 0:1]).then_inc(row_ready, 1)
            dve.wait_ge(rows_in, 16)
            ch.link(v.tensor_scalar(rows, rows, limit_col[B, 0:1], None, ALU.is_lt))
            ch.link(v.tensor_reduce(found[B, 1:2], rows, AX.X, ALU.add))
            ch.link(v.scalar_tensor_tensor(out=found[B, 2:3], in0=found[B, 0:1], scalar=float(ECOLS),
                                           in1=found[B, 1:2], op0=ALU.mult, op1=ALU.add))
            v.tensor_copy(start_i[B, :], found[B, 2:3]).then_inc(start_ready, 1)

            def group(i, g):
                dve.wait_ge(xg_in[i], 8 * (g - i) + 16 + (16 if isinstance(g, int) and g == GROUPS - 1 else 0))
                dve.wait_ge(g_norm, g)
                plain()
                for t in range(GROUP):
                    last = v.bn_stats(gstats[:, t, :], xg[i][:, t, :])
                ch.link(last)
                plain()
                for t in range(GROUP):
                    last = v.bn_aggr(gmv[:, t, :], gstats[:, t, :])
                ch.link(last)
                v.tensor_copy(gvar[:, :], gmv[:, :, 1]).then_inc(g_var, 1)
                dve.wait_ge(g_std, g + 1)
                ch.link(v.reciprocal(grstd[:, i, :], gvar[:, :]))
                v.scalar_tensor_tensor(out=gshift[:, i, :], in0=gmv[:, :, 0], scalar=-1.0,
                                       in1=grstd[:, i, :], op0=ALU.mult, op1=ALU.mult).then_inc(g_stat, 1)
                dve.wait_ge(g_hi, g + 1)
                dve.wait_ge(g_mid, g)
                dve.wait_ge(g_lo, g)
                v.tensor_tensor(grest, xn[i], gparts[i][:, :, 0, :], ALU.subtract).then_inc(g_rest, 1)
                dve.wait_ge(g_mid, g + 1)
                v.tensor_tensor(gparts[i][:, :, 2, :], grest, gparts[i][:, :, 1, :],
                                ALU.subtract).then_inc(g_lo, 1)

            GL = 3
            ch0 = ch.n
            group(0, 0)
            group(1, 1)
            assert ch.n == ch0 + 2 * GL
            with dve.Fori(1, (GROUPS - 1) // 2) as g2:
                for i in range(2):
                    ch.begin(g2 * (2 * GL) + (ch0 + i * GL))
                    group(i, g2 * 2 + i)
            ch.begin(ch0 + GL * (GROUPS - 1))
            group(0, GROUPS - 1)

            dve.wait_ge(win_in, 32)
            v.tensor_scalar(win[:, 0, :], win[:, 0, :], limit_col[B, 0:1], None,
                            ALU.subtract).then_inc(win_rel, 1)
            for j in range(TILES // 2):
                dve.wait_ge(win_T, j + 1)
                for a in range(2):
                    k = 2 * j + a
                    pb = bank[4 + j % 2][:, a * 256:a * 256 + BLOCKS]
                    pi = bank[4 + j % 2][:, a * 256 + P:a * 256 + P + BLOCKS]
                    v.tensor_scalar(rel_all[:, :, k], pb, float(-R * WIN[k][0]), None, ALU.add)
                    last = v.tensor_copy(idx_all[:, :, k], pi)
                last.then_inc(win_copied, 1)
            dve.wait_ge(win_copied, TILES // 2)
            ch.begin(ch.base + ch.n)
            ch.link(v.tensor_scalar(in_window, rel_all, 0.0, None, ALU.is_ge))
            for k in range(TILES):
                last = v.scalar_tensor_tensor(out=in_window[:, :, k], in0=rel_all[:, :, k],
                                              scalar=float(HOT_AT[k + 1] - HOT_AT[k]), in1=in_window[:, :, k],
                                              op0=ALU.is_lt, op1=ALU.mult)
            ch.link(last)
            v.tensor_reduce(found[:, 3:4], in_window, AX.XY, ALU.add).then_inc(matched, 1)
            dve.wait_ge(matched_sum, 1)
            v.tensor_scalar(general_i[:, :], C[0:1, 0:1], float(E), None, ALU.is_lt).then_inc(general_known, 1)
            v.memset(idle[:, :], 0.0).then_inc(tables_ready, 1)
            general = is_general(dve)

            def general_sums(layer):
                dve.wait_ge(below_made, layer + 1)
                with dve.Fori(0, STEPS) as i:
                    n = i + layer * STEPS
                    chg.begin(n * 3)
                    dve.wait_ge(edge_in, n * 32 + 32)
                    v.tensor_copy(g_src, g_srcf).then_inc(edge_idx, 1)
                    dve.wait_ge(key_row, n + 1)
                    chg.link(v.tensor_scalar(same, T[:, 0:P], g_key, None, ALU.is_equal))
                    chg.link(v.tensor_tensor(before_me, same, below, ALU.mult))
                    v.tensor_reduce(g_tmp[:, 0:1], before_me, AX.X, ALU.add).then_inc(same_ready, 1)
                    dve.wait_ge(same_ready, n + 1)
                    v.tensor_scalar(g_tmp[:, 1:2], g_tmp[:, 0:1], 0.5, None, ALU.is_lt)
                    chg.link(v.tensor_tensor(g_tmp[:, 2:3], g_key, spare_row, ALU.subtract))
                    v.scalar_tensor_tensor(out=g_dest, in0=g_tmp[:, 2:3], scalar=g_tmp[:, 1:2], in1=spare_row,
                                           op0=ALU.mult, op1=ALU.add).then_inc(dest_ready, 1)
                    dve.wait_ge(edge_sum, n + 1)
                    v.tensor_copy(g_sum, T2[:, 0:MCOLS]).then_inc(edge_sum_out, 1)
                    assert chg.n == 3

            def relations(layer):
                dve.wait_ge(basis_in[layer], 16 * (layer + 1))
                for b in range(NBASIS):
                    for r in range(R):
                        s = comp_sb[layer][:, r * NBASIS + b:r * NBASIS + b + 1]
                        if b == 0:
                            last = v.tensor_scalar(wrel[:, r, :, :], basis[:, b, :, :], s, None, ALU.mult)
                        else:
                            last = v.scalar_tensor_tensor(out=wrel[:, r, :, :], in0=basis[:, b, :, :], scalar=s,
                                                          in1=wrel[:, r, :, :], op0=ALU.mult, op1=ALU.add)
                    ch.link(last) if b < NBASIS - 1 else last.then_inc(s_wrel, 1)

            def one_hots(h, G):
                with dve.If(general):
                    pass
                with dve.Else():
                    one_hots_fast(h, G)

            def one_hots_fast(h, G):
                dve.wait_ge(idx_in[h], G * 32 + 32)
                summed(dve, G, h, back=2)
                for k in range(TILES):
                    w = HOT_AT[k + 1] - HOT_AT[k]
                    last = v.tensor_scalar(hot[:, h, HOT_AT[k]:HOT_AT[k + 1]], iota_b[:, 0:w],
                                           rel[:, h, k:k + 1], None, ALU.is_equal)
                last.then_inc(hot_ready, 1)

            def scale(layer, h, G, p):
                summed(dve, G, h)
                iv = inv[:, h, :]
                if layer == 0:
                    dve.wait_ge(inv_out, p * 16)
                    ch.link(v.tensor_scalar(iv, C[:, :], 1.0, None, ALU.max))
                    ch.link(v.reciprocal(iv, iv))
                else:
                    dve.wait_ge(inv_in[h], p * 16 + 16)
                dve.wait_ge(tr_done, G)
                for k in range(HALVES):
                    last = v.tensor_tensor(
                        scaled[:, k, :, h * BD:(h + 1) * BD].rearrange("p r n -> p n r"),
                        S[k][:, :].rearrange("p (n r) -> p n r", r=R),
                        iv.rearrange("p (n r) -> p n r", r=R), ALU.mult)
                last.then_inc(sc_ready, 1)

            def save(p):
                dve.wait_ge(relu_done, START + p + 1)
                v.tensor_copy(featT[:, :, bass.ds(p * P, P)], hcur[:, :, :]).then_inc(feat_saved, 1)
                dve.wait_ge(hi_done, p + 1)
                dve.wait_ge(mid_done, START + p)
                dve.wait_ge(lo_done, START + p)
                v.tensor_tensor(rest[:, :], T2[:, 0:D], parts[:, 0, :], ALU.subtract).then_inc(rest_done, 1)
                dve.wait_ge(mid_done, START + p + 1)
                v.tensor_tensor(parts[:, 2, :], rest[:, :], parts[:, 1, :], ALU.subtract).then_inc(lo_done, 1)

            def layer_norm(dst_, src_, count):
                plain()
                ch.link(v.bn_stats(stats[:, :], src_))
                plain()
                v.bn_aggr(mv[:, :], stats[:, :]).then_inc(ln_var, 1)
                dve.wait_ge(ln_std, count)
                ch.link(v.reciprocal(rstd[:, :], std[:, :]))
                return v.tensor_scalar(dst_, src_, mv[:, 0:1], rstd[:, 0:1], ALU.subtract, ALU.mult)

            def typed(p):
                dve.wait_ge(node_in, p * 48 + 48)
                v.tensor_scalar(tmask[:, :], iota8[:, 0:TYPES], ntcol[:, 0:1], None, ALU.is_equal)
                v.tensor_scalar(tmaskT[:, :], ntrow[:, :], pid[0:TYPES, 0:1], None,
                                ALU.is_equal).then_inc(mask_done, 1)
                dve.wait_ge(mask_done, p + 1)
                dve.wait_ge(o_done, START + p)
                for j in range(TYPES + 1):
                    dve.wait_ge(lin_ps, p * 6 + j + 1)
                    acc = xcur if j == 0 else x1
                    s = tmask[:, j:j + 1] if j < TYPES else 1.0
                    v.scalar_tensor_tensor(out=x1[:, :], in0=YP[j % 2][:, 0:D], scalar=s, in1=acc[:, :],
                                           op0=ALU.mult, op1=ALU.add).then_inc(lin_acc, 1)
                    dve.wait_ge(lin_acc, START + p * 6 + j + 1)
                dve.wait_ge(znT_done, START + p)
                ch.link(layer_norm(zn[:, :], x1[:, :], p * 2 + 1))
                layer_norm(zn[:, :], zn[:, :], p * 2 + 2).then_inc(zn_done, 1)

            def route(p):
                dve.wait_ge(lg_done, p + 1)
                v.tensor_copy(lg[:, :], T[:, 0:EXPERTS]).then_inc(lg_read, 1)
                dve.wait_ge(lg_read, p + 1)
                plain()
                ch.link(v.max(top[:, :], lg[:, :]))
                plain()
                ch.link(v.max_index(topi[:, :], top[:, :], lg[:, :]))
                v.tensor_copy(topf[:, :], topi[:, 0:2])
                v.tensor_tensor(soft[:, 0:1], top[:, 0:1], top[:, 1:2], ALU.subtract).then_inc(margin_done, 1)
                dve.wait_ge(tanh_done, p + 1)
                v.tensor_scalar(soft[:, 2:3], soft[:, 1:2], 0.5, 0.5, ALU.mult, ALU.add)
                ch.link(v.tensor_scalar(soft[:, 3:4], soft[:, 1:2], -0.5, 0.5, ALU.mult, ALU.add))
                v.tensor_scalar(wfull[:, 0, :], iota8[:, :], topf[:, 0:1], soft[:, 2:3], ALU.is_equal, ALU.mult)
                ch.link(v.tensor_scalar(wfull[:, 1, :], iota8[:, :], topf[:, 1:2], soft[:, 3:4],
                                        ALU.is_equal, ALU.mult))
                v.tensor_tensor(wfull[:, 0, :], wfull[:, 0, :], wfull[:, 1, :], ALU.add).then_inc(wf_done, 1)
                dve.wait_ge(wf_done, p + 1)

            def mix(p):
                for e in range(EXPERTS):
                    dve.wait_ge(y_ps, p * EXPERTS + e + 1)
                    acc = x1 if e == 0 else o
                    v.scalar_tensor_tensor(out=o[:, :], in0=YP[e % 2][:, 0:D], scalar=wfull[:, 0, e:e + 1],
                                           in1=acc[:, :], op0=ALU.mult, op1=ALU.add).then_inc(y_acc, 1)
                    dve.wait_ge(y_acc, p * EXPERTS + e + 1)
                dve.wait_ge(b2_ps, p + 1)
                v.tensor_tensor(o[:, :], o[:, :], T[:, 0:D], ALU.add).then_inc(o_done, 1)

            def layer_steps(layer):
                g0 = layer * PAIRS
                one_hots(0, g0)
                one_hots(1, g0)
                scale(layer, 0, g0, 0)
                one_hots(0, g0 + 1)
                scale(layer, 1, g0, 0)
                one_hots(1, g0 + 1)
                base = ch.base + ch.n

                def body(p, more=True):
                    G = p + g0
                    scale(layer, 0, G, p)
                    if more:
                        one_hots(0, G + 1)
                    if layer == 0:
                        scale(layer, 1, G, p)
                        if more:
                            one_hots(1, G + 1)
                        save(p - 1)
                    else:
                        typed(p - 1)
                        scale(layer, 1, G, p)
                        if more:
                            one_hots(1, G + 1)
                        route(p - 1)
                        mix(p - 1)

                per = 4 if layer == 0 else 5 + 4
                with dve.Fori(1, PAIRS - 1) as p:
                    ch.begin(p * per + (base - per))
                    body(p)
                    assert ch.n == per, ch.n
                ch.begin(base + per * (PAIRS - 2))
                body(PAIRS - 1, more=False)
                if layer == 0:
                    save(PAIRS - 1)
                else:
                    typed(PAIRS - 1)
                    route(PAIRS - 1)
                    mix(PAIRS - 1)

            dve.wait_ge(weights_in, 16 * N_WEIGHTS)
            dve.wait_ge(tables_out, 32)
            with dve.If(general):
                general_sums(0)
            relations(0)
            layer_steps(0)
            with dve.If(general):
                general_sums(1)
            relations(1)
            layer_steps(1)

        @block.tensor
        def _(pe):
            t = nc.tensor
            pe.wait_ge(s_const, 3)
            pe.wait_ge(s_before, 1)
            t.matmul(T[0:BLOCKS, 0:1], before[0:EROWS, :], ones_f[0:EROWS, 0:1], start=True,
                     stop=True).then_inc(s_count, 1)

            def turn_group(i, g):
                pe.wait_ge(g_norm, g + 1)
                pe.wait_ge(g_Tc, g)
                for j in range(4):
                    n = min(4, 2 * GROUP - 4 * j) // 2
                    for k in range(HALVES):
                        for a in range(n):
                            last = t.transpose(bank[j][:, (k * n + a) * P:(k * n + a + 1) * P],
                                               xn[i][:, 2 * j + a, k * P:(k + 1) * P], ident[:, :])
                    last.then_inc(g_T, 1)

            pe.wait_ge(row_ready, 1)
            turn_group(0, 0)
            turn_group(1, 1)
            with pe.Fori(1, (GROUPS - 1) // 2) as g2:
                for i in range(2):
                    turn_group(i, g2 * 2 + i)
            turn_group(0, GROUPS - 1)

            pe.wait_ge(win_rel, 1)
            for j in range(TILES // 2):
                if j >= 2:
                    pe.wait_ge(win_copied, j - 1)
                for a in range(2):
                    k = 2 * j + a
                    t.transpose(bank[4 + j % 2][:, a * 256:a * 256 + BLOCKS], win[:, 0, k * P:(k + 1) * P],
                                ident[0:BLOCKS, 0:BLOCKS])
                    last = t.transpose(bank[4 + j % 2][:, a * 256 + P:a * 256 + P + BLOCKS],
                                       win[:, 1, k * P:(k + 1) * P], ident[0:BLOCKS, 0:BLOCKS])
                last.then_inc(win_T, 1)
            pe.wait_ge(win_copied, TILES // 2)

            pe.wait_ge(matched, 1)
            t.matmul(C[0:1, 0:1], found[:, 3:4], ones_f[:, 0:1], start=True, stop=True).then_inc(matched_sum, 1)
            general = is_general(pe)

            def general_sums(layer):
                with pe.Fori(0, STEPS) as i:
                    n = i + layer * STEPS
                    pe.wait_ge(edge_in, n * 32 + 32)
                    t.matmul(T[:, 0:P], g_key.broadcast_to([P, P]), ident[:, :], start=True,
                             stop=True).then_inc(key_row, 1)
                    pe.wait_ge(same_ready, n + 1)
                    pe.wait_ge(edge_rows, n * 16 + 16)
                    t.matmul(T2[:, D:MCOLS], same, ones_b[:, 0:1], start=True, stop=True)
                    for q in range(PARTS):
                        last = t.matmul(T2[:, 0:D], same, g_rows[:, q * D:(q + 1) * D], start=(q == 0),
                                        stop=(q == PARTS - 1))
                    last.then_inc(edge_sum, 1)

            def aggregate(layer, h, G):
                pe.wait_ge(sc_ready, G * 2 + h)
                with pe.If(general):
                    pe.wait_ge(sums_in[h], G * 16 + 16)
                    for q in range(QUADS):
                        at = slice(q * P, (q + 1) * P)
                        if layer == 0:
                            t.matmul(C[:, at], sums_sb[h][:, q, D:MCOLS].broadcast_to([P, P]), ident[:, :],
                                     start=True, stop=True)
                        for f in range(HALVES):
                            last = t.transpose(S[f][:, at], sums_sb[h][:, q, f * P:(f + 1) * P], ident[:, :])
                    last.then_inc(used[TILES - 1], 1)
                with pe.Else():
                    aggregate_fast(layer, h, G)

            def aggregate_fast(layer, h, G):
                pe.wait_ge(hot_ready, G * 2 + h + 1)
                full = pe.snap(G * 32 + (h * 16 + 16)) if not isinstance(G, int) else G * 32 + h * 16 + 16
                for k in range(TILES):
                    lo, hi = WIN[k]
                    oh = hot[:, h, HOT_AT[k]:HOT_AT[k + 1]]
                    pe.wait_ge(gathered[k], full)
                    if layer == 0:
                        t.matmul(C[:, R * lo:R * hi], ones_b[:, :], oh, start=(k == 0), stop=(k == TILES - 1),
                                 skip_group_check=True)
                    for f in range(HALVES):
                        for q in range(PARTS):
                            last = t.matmul(S[f][:, R * lo:R * hi],
                                            slot[:, k, q * D + f * P:q * D + (f + 1) * P], oh,
                                            start=(k == 0 and q == 0), stop=(k == TILES - 1 and q == PARTS - 1),
                                            skip_group_check=True)
                    if k % RUN == RUN - 1:
                        last.then_inc(used[k], 1)

            def transform(layer, G, p):
                pe.wait_ge(sc_ready, G * 2 + 2)
                if layer == 0:
                    pe.wait_ge(relu_done, START + p)
                else:
                    pe.wait_ge(o_done, START + p)
                for o_ in range(HALVES):
                    n = 0
                    for k in range(HALVES):
                        t.matmul(T[:, o_ * P:(o_ + 1) * P], root_sb[:, k, o_ * P:(o_ + 1) * P],
                                 featT[:, k, bass.ds(p * P, P)], start=(k == 0), stop=False)
                        for r in range(R):
                            n += 1
                            last = t.matmul(T[:, o_ * P:(o_ + 1) * P], wrel[:, r, k, o_ * P:(o_ + 1) * P],
                                            scaled[:, k, r, :], start=False, stop=(n == R * HALVES))
                last.then_inc(tr_done, 1)

            def turn(p):
                pe.wait_ge(relu_done, START + p + 1)
                pe.wait_ge(rest_done, START + p)
                for k in range(HALVES):
                    last = t.transpose(T2[:, k * P:(k + 1) * P], hcur[:, k, :], ident[:, :])
                last.then_inc(hT_done, 1)

            def typed(p):
                pe.wait_ge(relu_done, START + p + (PAIRS + 1))
                pe.wait_ge(mask_done, p + 1)
                for j in range(TYPES + 1):
                    if j >= 2:
                        pe.wait_ge(lin_acc, START + p * 6 + (j - 1))
                    Y = YP[j % 2][:, 0:D]
                    if j < TYPES:
                        t.matmul(Y, hcur[:, 0, :], linw_sb[:, j, 0, :], start=True, stop=False)
                        last = t.matmul(Y, hcur[:, 1, :], linw_sb[:, j, 1, :], start=False, stop=True)
                    else:
                        last = t.matmul(Y, tmaskT[:, :], linb_sb[:, :], start=True, stop=True)
                    last.then_inc(lin_ps, 1)

            def experts(p):
                pe.wait_ge(zn_done, p + 1)
                for k in range(HALVES):
                    last = t.transpose(T2[:, k * P:(k + 1) * P], zn[:, k * P:(k + 1) * P], ident[:, :])
                last.then_inc(znT_done, 1)
                pe.wait_ge(xnT_done, p + 1)
                for k in range(HALVES):
                    t.matmul(T[:, 0:EXPERTS], xnT[:, k, :], wr_sb[:, k, :], start=(k == 0), stop=False)
                t.matmul(T[:, 0:EXPERTS], ones_f[0:1, :], br_sb[:, :], start=False, stop=True).then_inc(lg_done, 1)

                def up(e):
                    if e >= 2:
                        pe.wait_ge(h_act, p * EXPERTS + (e - 1))
                    for c in range(HCH):
                        for k in range(HALVES):
                            last = t.matmul(HP[e % 2][:, c * P:(c + 1) * P], w1_sb[:, e, k, c * P:(c + 1) * P],
                                            xnT[:, k, :], start=(k == 0), stop=(k == HALVES - 1))
                    last.then_inc(h_ps, 1)

                def down(e):
                    pe.wait_ge(h_act, p * EXPERTS + (e + 1))
                    if e >= 2:
                        pe.wait_ge(y_acc, p * EXPERTS + (e - 1))
                    else:
                        pe.wait_ge(lin_acc, START + p * 6 + 6)
                    for c in range(HCH):
                        last = t.matmul(YP[e % 2][:, 0:D], act[:, e % 2, c, :], w2_sb[:, e, c, :],
                                        start=(c == 0), stop=(c == HCH - 1))
                    last.then_inc(y_ps, 1)

                up(0)
                up(1)
                for e in range(EXPERTS):
                    down(e)
                    if e + 2 < EXPERTS:
                        up(e + 2)
                    if e == 1:
                        pe.wait_ge(wf_done, p + 1)
                        t.transpose(T2[0:EXPERTS, 256:256 + P], wfull[:, 0, :], ident[:, :]).then_inc(wfT_ps, 1)
                    if e == 5:
                        pe.wait_ge(wfT_done, p + 1)
                        t.matmul(T[:, 0:D], wfT[:, :], b2_sb[:, :], start=True, stop=True).then_inc(b2_ps, 1)

            pe.wait_ge(g_Tc, GROUPS)
            pe.wait_ge(weights_in, 16 * N_WEIGHTS)
            with pe.If(general):
                general_sums(0)
            aggregate(0, 0, 0)
            aggregate(0, 1, 0)
            pe.wait_ge(s_wrel, 1)
            with pe.Fori(1, PAIRS) as p:
                aggregate(0, 0, p)
                transform(0, p - 1, p - 1)
                aggregate(0, 1, p)
                turn(p - 1)
            transform(0, PAIRS - 1, PAIRS - 1)
            turn(PAIRS - 1)
            with pe.If(general):
                general_sums(1)
            aggregate(1, 0, PAIRS)
            aggregate(1, 1, PAIRS)
            pe.wait_ge(s_wrel, 2)
            pe.wait_ge(basis_in[1], 32)
            pe.wait_ge(ffn_in, 48)
            pe.wait_ge(feat_saved, PAIRS)
            with pe.Fori(1, PAIRS) as p:
                aggregate(1, 0, p + PAIRS)
                transform(1, p + (PAIRS - 1), p - 1)
                typed(p - 1)
                aggregate(1, 1, p + PAIRS)
                experts(p - 1)
            transform(1, 2 * PAIRS - 1, PAIRS - 1)
            typed(PAIRS - 1)
            experts(PAIRS - 1)


_INS = ['x', 'src', 'dst', 'edge_type_8', 'node_type_5', 'L0_gnn_basis0', 'L0_gnn_comp0', 'L0_gnn_root0',
        'L0_gnn_bias0', 'L0_gnn_basis1', 'L0_gnn_comp1', 'L0_gnn_root1', 'L0_gnn_bias1', 'L0_gnn_lin_w',
        'L0_gnn_lin_b', 'L0_ffn_gamma', 'L0_ffn_beta', 'L0_ffn_Wr', 'L0_ffn_br', 'L0_ffn_W1', 'L0_ffn_b1',
        'L0_ffn_W2', 'L0_ffn_b2']


def kernel(**inputs):
    import numpy as _np
    import concourse.bacc as _bacc
    from concourse import mybir as _mybir
    from concourse.bass_utils import run_bass_kernel_spmd as _run

    nc = _bacc.Bacc("TRN2", target_bir_lowering=False, num_devices=1)
    arrays, args = {}, []
    for name in _INS:
        a = _np.ascontiguousarray(inputs[name])
        arrays[f"in_{name}_dram"] = a
        args.append(nc.dram_tensor(f"in_{name}_dram", a.shape, _mybir.dt.from_np(a.dtype), kind="ExternalInput").ap())
    args.append(nc.dram_tensor("out_0_dram", (N, D), _mybir.dt.float32, kind="ExternalOutput").ap())
    build(nc, *args)
    r = _run(nc, [arrays], core_ids=[0])
    return r.results[0]["out_0_dram"]
```

```python
from contextlib import ExitStack
import math

import concourse.bass as bass
from concourse import mybir

ALU = mybir.AluOpType
ACT = mybir.ActivationFunctionType
AX = mybir.AxisListType
F32 = mybir.dt.float32
BF16 = mybir.dt.bfloat16
I32 = mybir.dt.int32
U32 = mybir.dt.uint32

P = 128
N, D, E, R, NBASIS, TYPES = 6250, 256, 206250, 8, 4, 5
EXPERTS, HID = 8, 512
EPS = 1e-5
HALVES = D // P
HCH = HID // P
BD = 64
SLOTS = BD * R
BLOCKS = -(-N // BD)
PAIRS = -(-N // P)
NPAD = PAIRS * P
LAST = N - (PAIRS - 1) * P
MEAN = E / N
START = 1
RUN = 3
TILES = 18
CAP = TILES * P
EROWS, ECOLS = 125, E // 125
EWINDOWS = E // CAP + 2
PADLEN, PADROWS = EWINDOWS * CAP - E, 6
PADKEY = float(BLOCKS * SLOTS)
GROUP = 7
GROUPS = PAIRS // GROUP
PARTS = 3
MROWS = (BLOCKS + 1) * SLOTS
SPARE = BLOCKS * SLOTS + P
MIXES = R * NBASIS
STEPS = -(-E // P)
QUADS = SLOTS // P
MCOLS = D + 1


def tile_windows():
    out = []
    for k in range(TILES):
        a, b = P * k / MEAN, (P * k + P - 1) / MEAN
        spread = 4.5 * math.sqrt(MEAN - 1) / MEAN
        out.append((max(0, math.floor(a - spread * math.sqrt(a) - 0.5)),
                    min(BD, math.ceil(b + spread * math.sqrt(b) + 0.5) + 1)))
    return out


WIN = tile_windows()
HOT_AT = [R * sum(hi - lo for lo, hi in WIN[:k]) for k in range(TILES + 1)]
HOT_MAX = R * max(hi - lo for lo, hi in WIN)


class Chain:

    def __init__(self, eng, sem):
        self.eng, self.sem, self.base, self.n = eng, sem, 0, 0

    def begin(self, base):
        self.base, self.n = base, 0

    def link(self, ins):
        self.n += 1
        ins.then_inc(self.sem, 1)
        self.eng.wait_ge(self.sem, self.base + self.n)


def build(nc, x, src, dst, etype, ntype, basis0, comp0, root0, bias0, basis1, comp1, root1, bias1,
          lin_w, lin_b, gamma, beta, Wr, br, W1, b1, W2, b2, out):
    with ExitStack() as ctx:
        def sb(name, shape, dt):
            return ctx.enter_context(nc.sbuf_tensor(name, shape, dt))

        def sem(name):
            return ctx.enter_context(nc.semaphore(name))

        def dram(name, shape, dt):
            return nc.dram_tensor(name, shape, dt, kind="Internal").ap()

        key_d = dram("key_d", (EWINDOWS * CAP,), F32)
        src_d = dram("src_d", (EWINDOWS * CAP,), F32)
        table = [dram("table0", (NPAD, PARTS * D), BF16), dram("table1", (NPAD, PARTS * D), BF16)]
        idx_d = dram("idx_d", (P, BLOCKS, TILES), I32)
        rel_d = dram("rel_d", (P, BLOCKS, TILES), F32)
        inv_d = dram("inv_d", (BLOCKS, SLOTS), F32)

        sums_d = dram("sums_d", (MROWS, MCOLS), F32)

        featT = sb("featT", [P, HALVES, NPAD], F32)
        slot = sb("slot", [P, TILES, PARTS * D], BF16)
        basis_sb = sb("basis_sb", [P, NBASIS, HALVES, D], F32)
        mixed = sb("mixed", [P, NBASIS, HALVES, P], F32)
        scaled = sb("scaled", [P, HALVES, R, P], F32)
        ffn_w = sb("ffn_w", [P, HALVES * EXPERTS * HID + EXPERTS * HCH * D], F32)
        w1_sb = ffn_w[:, 0:HALVES * EXPERTS * HID].rearrange("p (e k h) -> p e k h", e=EXPERTS, k=HALVES)
        w2_sb = ffn_w[:, HALVES * EXPERTS * HID:].rearrange("p (e c d) -> p e c d", e=EXPERTS, c=HCH)
        linw_sb = sb("linw_sb", [P, TYPES, HALVES, D], F32)
        root_sb = sb("root_sb", [P, HALVES, D], F32)
        wr_sb = sb("wr_sb", [P, HALVES, EXPERTS], F32)
        small = sb("small", [P, 96], F32)
        bias_sb = [small[:, 0:2], small[:, 2:4]]
        gamma_sb, beta_sb = small[:, 4:6], small[:, 6:8]
        b1_sb = small[:, 8:40]
        comp_sb = [small[:, 40:72], sb("comp1_sb", [P, R * NBASIS], F32)[:, :]]
        linb_sb = sb("linb_sb", [TYPES, D], F32)
        b2_sb = sb("b2_sb", [EXPERTS, D], F32)
        br_sb = sb("br_sb", [1, EXPERTS], F32)
        ident = sb("ident", [P, P], F32)
        ones_b = sb("ones_b", [P, P], BF16)
        ones_f = sb("ones_f", [P, P], F32)
        iota_b = sb("iota_b", [P, HOT_MAX], BF16)
        iota8 = sb("iota8", [P, EXPERTS], F32)
        pid = sb("pid", [P, 1], F32)
        hot = sb("hot", [P, 2, HOT_AT[TILES]], BF16)
        idx = sb("idx", [P, 2, TILES], I32)
        rel = sb("rel", [P, 2, TILES], F32)
        inv = sb("inv", [P, 2, SLOTS], F32)
        hcur = sb("hcur", [P, HALVES, P], F32)
        parts = sb("parts", [P, PARTS, D], BF16)
        rest = sb("rest", [P, D], F32)
        xcur = sb("xcur", [P, D], F32)
        ntcol = sb("ntcol", [P, 1], I32)
        ntrow = sb("ntrow", [TYPES, P], I32)
        tmask = sb("tmask", [P, TYPES], F32)
        tmaskT = sb("tmaskT", [TYPES, P], F32)
        x1 = sb("x1", [P, D], F32)
        zn = sb("zn", [P, D], F32)
        stats = sb("stats", [P, 6], F32)
        mv = sb("mv", [P, 2], F32)
        rstd = sb("rstd", [P, 1], F32)
        idle = sb("idle", [P, 1], F32)
        std = sb("std", [P, 1], F32)
        xnT = sb("xnT", [P, HALVES, P], F32)
        lg = sb("lg", [P, EXPERTS], F32)
        top = sb("top", [P, 8], F32)
        topi = sb("topi", [P, 8], U32)
        topf = sb("topf", [P, 2], F32)
        soft = sb("soft", [P, 4], F32)
        wfull = sb("wfull", [P, 2, EXPERTS], F32)
        wfT = sb("wfT", [EXPERTS, P], F32)
        act = sb("act", [P, 2, HCH, P], F32)
        o = sb("o", [P, D], F32)

        def carve(t, at, n):
            return t[:, at:at + n]
        GW = GROUP * D
        xg = [carve(ffn_w, i * GW, GW).rearrange("p (t d) -> p t d", t=GROUP) for i in range(2)]
        xn = [carve(ffn_w, (2 + i) * GW, GW).rearrange("p (t d) -> p t d", t=GROUP) for i in range(2)]
        grest = carve(ffn_w, 4 * GW, GW).rearrange("p (t d) -> p t d", t=GROUP)
        gparts = [carve(ffn_w, 5 * GW + i * PARTS * GW // 2, PARTS * GW // 2).bitcast(BF16).rearrange(
            "p (t q d) -> p t q d", t=GROUP, q=PARTS) for i in range(2)]
        gvar = sb("gvar", [P, GROUP], F32)
        eps_col = sb("eps_col", [P, 1], F32)
        gstats = sb("gstats", [P, GROUP, 6], F32)
        gmv = sb("gmv", [P, GROUP, 2], F32)
        grstd = sb("grstd", [P, 2, GROUP], F32)
        gshift = sb("gshift", [P, 2, GROUP], F32)
        early = slot[:, :, :].rearrange("p t d -> p (t d)").bitcast(F32)
        raw = early[0:EROWS, 0:3 * ECOLS].bitcast(I32).rearrange("p (a c) -> p a c", a=3)
        win = early[0:BLOCKS, 0:2 * CAP].rearrange("p (a c) -> p a c", a=2)
        late = scaled[:, :, :, :].rearrange("p a r n -> p (a r n)")
        edge_f = [late[0:EROWS, 0:ECOLS],
                  basis_sb[:, :, :, :].rearrange("p b k d -> p (b k d)")[0:EROWS, 0:ECOLS]]
        rows = linw_sb[:, :, :, :].rearrange("p t k d -> p (t k d)")[0:BLOCKS, 0:ECOLS]
        idx_all = carve(ffn_w, 5 * GW + PARTS * GW, BLOCKS * TILES).bitcast(I32).rearrange(
            "p (b t) -> p b t", t=TILES)
        rel_all = hot[:, :, :].rearrange("p a c -> p (a c)").bitcast(F32)[:, 0:BLOCKS * TILES].rearrange(
            "p (b t) -> p b t", t=TILES)
        padt = [inv[0:PADROWS, :, :].rearrange("p a c -> p (a c)")[:, 0:PADLEN // PADROWS],
                act[0:PADROWS, :, :, :].rearrange("p a c n -> p (a c n)")[:, 0:PADLEN // PADROWS]]
        limit_col = sb("limit_col", [P, 1], F32)
        limit_row = x1[:, 0:BLOCKS]
        before = x1[:, P:P + BLOCKS]
        found = sb("found", [P, 4], F32)
        in_last, up_to = zn[:, 0:BLOCKS], zn[:, P:P + BLOCKS]
        row_i = sb("row_i", [P, 1], I32)
        start_i = sb("start_i", [P, 1], I32)

        MW = QUADS * MCOLS
        sums_sb = [carve(early, i * MW, MW).rearrange("p (q c) -> p q c", q=QUADS) for i in range(2)]
        zeros = carve(early, 2 * MW, MW)
        g_rows = carve(early, 3 * MW, PARTS * D // 2).bitcast(BF16)
        g_sum = carve(early, 3 * MW + 384, MCOLS)
        same = carve(early, 3 * MW + 648, P // 2).bitcast(BF16)
        below = carve(early, 3 * MW + 712, P)
        before_me = carve(early, 3 * MW + 840, P)
        g_key = carve(early, 3 * MW + 968, 1)
        g_srcf = carve(early, 3 * MW + 969, 1)
        g_src = carve(early, 3 * MW + 970, 1).bitcast(I32)
        g_dest = carve(early, 3 * MW + 971, 1).bitcast(I32)
        g_tmp = carve(early, 3 * MW + 972, 3)
        spare_row = carve(early, 3 * MW + 975, 1)
        in_window = carve(early, 2 * CAP, BLOCKS * TILES).rearrange("p (b t) -> p b t", t=TILES)
        general_i = sb("general_i", [1, 1], I32)
        last_tile = sb("last_tile", [1, BLOCKS], I32)
        last_count = sb("last_count", [1, 2, BLOCKS], I32)

        bank = [ctx.enter_context(nc.psum_tensor(f"bank{i}", [P, 512], F32)) for i in range(8)]
        S = bank[0:2]
        T, T2, C = bank[2], bank[3], bank[4]
        HP = bank[4:6]
        YP = bank[6:8]

        raw_in = [sem(f"raw_in{i}") for i in range(3)]
        s_const = sem("s_const")
        weights_in = sem("weights_in")
        basis_in = [sem(f"basis_in{i}") for i in range(2)]
        ffn_in = sem("ffn_in")
        edges_f = sem("edges_f")
        edges_out = sem("edges_out")
        s_before = sem("s_before")
        s_count = sem("s_count")
        row_ready = sem("row_ready")
        rows_in = sem("rows_in")
        start_ready = sem("start_ready")
        win_in = sem("win_in")
        win_rel = sem("win_rel")
        win_T = sem("win_T")
        win_copied = sem("win_copied")
        tables_ready = sem("tables_ready")
        same_ready = sem("same_ready")
        s_general = sem("s_general")
        tables_out = sem("tables_out")
        pool_waited = sem("pool_waited")
        sp_waited = sem("sp_waited")
        s_dve = sem("s_dve")
        mixed_ready = sem("mixed_ready")
        xg_in = [sem(f"xg_in{i}") for i in range(2)]
        g_stat = sem("g_stat")
        g_norm = sem("g_norm")
        g_var = sem("g_var")
        g_std = sem("g_std")
        ln_var = sem("ln_var")
        ln_std = sem("ln_std")
        margin_done = sem("margin_done")
        tanh_done = sem("tanh_done")
        g_hi = sem("g_hi")
        g_rest = sem("g_rest")
        g_mid = sem("g_mid")
        g_lo = sem("g_lo")
        g_T = sem("g_T")
        g_Tc = sem("g_Tc")
        g_out = [sem(f"g_out{i}") for i in range(2)]
        idx_in = [sem(f"idx_in{i}") for i in range(2)]
        gathered = [sem(f"gathered{k}") for k in range(TILES)]
        used = {k: sem(f"used{k}") for k in range(RUN - 1, TILES, RUN)}
        hot_ready = sem("hot_ready")
        sc_ready = sem("sc_ready")
        tr_done = sem("tr_done")
        relu_done = sem("relu_done")
        hT_done = sem("hT_done")
        feat_saved = sem("feat_saved")
        hi_done = sem("hi_done")
        rest_done = sem("rest_done")
        mid_done = sem("mid_done")
        lo_done = sem("lo_done")
        parts_out = sem("parts_out")
        inv_out = sem("inv_out")
        inv_in = [sem(f"inv_in{i}") for i in range(2)]
        node_in = sem("node_in")
        mask_done = sem("mask_done")
        lin_ps = sem("lin_ps")
        lin_acc = sem("lin_acc")
        zn_done = sem("zn_done")
        znT_done = sem("znT_done")
        xnT_done = sem("xnT_done")
        lg_done = sem("lg_done")
        lg_read = sem("lg_read")
        wf_done = sem("wf_done")
        wfT_ps = sem("wfT_ps")
        wfT_done = sem("wfT_done")
        h_ps = sem("h_ps")
        h_act = sem("h_act")
        y_ps = sem("y_ps")
        y_acc = sem("y_acc")
        b2_ps = sem("b2_ps")
        b2_added = sem("b2_added")
        out_done = sem("out_done")
        N_WEIGHTS = 12
        matched = sem("matched")
        matched_sum = sem("matched_sum")
        last_known = sem("last_known")
        last_summed = sem("last_summed")
        general_known = sem("general_known")
        zeros_made = sem("zeros_made")
        below_made = sem("below_made")
        sums_cleared = sem("sums_cleared")
        edge_in = sem("edge_in")
        edge_idx = sem("edge_idx")
        key_row = sem("key_row")
        dest_ready = sem("dest_ready")
        edge_rows = sem("edge_rows")
        edge_sum = sem("edge_sum")
        edge_sum_out = sem("edge_sum_out")
        added = sem("added")
        sums_in = [sem(f"sums_in{i}") for i in range(2)]

        def summed(eng, G, h, back=0):
            eng.wait_ge(used[TILES - 1], G * 2 + (START + h + 1 - back))

        def is_general(eng):
            eng.wait_ge(general_known, 1)
            return eng.value_load(general_i[0:1, 0:1], min_val=0, max_val=1)

        block = ctx.enter_context(nc.Block())

        x_g = x[0:(GROUPS - 1) * GROUP * P, :].rearrange("(g t p) d -> g p t d", t=GROUP, p=P)
        tab_g = table[0].rearrange("(g t p) d -> g p t d", t=GROUP, p=P)
        tab_p = table[1].rearrange("(g p) d -> g p d", p=P)
        inv_p = inv_d.rearrange("(g a) s -> g a s", a=2)

        @block.sync
        def _(sp):
            for q in (relu_done, rest_done, b2_added, mid_done, lo_done, znT_done, lin_acc, *used.values()):
                sp.sem_inc(q, START)
            for i, a in enumerate((dst, etype, src)):
                sp.dma_start(raw[:, i, :], a.rearrange("(p c) -> p c", p=EROWS)).then_inc(raw_in[i], 16)

            def load_group(i, g):
                if not isinstance(g, int) or g >= 2:
                    sp.wait_ge(g_norm, g - 1)
                if isinstance(g, int) and g == GROUPS - 1:
                    base = g * GROUP * P
                    sp.dma_start(xg[i][:, 0:GROUP - 1, :], x[base:base + (GROUP - 1) * P, :].rearrange(
                        "(t p) d -> p t d", p=P)).then_inc(xg_in[i], 16)
                    sp.dma_start(xg[i][0:LAST, GROUP - 1, :], x[N - LAST:N, :]).then_inc(xg_in[i], 16)
                else:
                    src_ap = x_g[g] if isinstance(g, int) else x_g[bass.ds(g, 1), :, :, :].rearrange(
                        "a p t d -> (a p) t d")
                    sp.dma_start(xg[i], src_ap).then_inc(xg_in[i], 16)

            load_group(0, 0)
            load_group(1, 1)
            sp.wait_ge(edges_f, 2)
            for i, a in enumerate((key_d, src_d)):
                sp.dma_start(a[0:E].rearrange("(p c) -> p c", p=EROWS), edge_f[i]).then_inc(edges_out, 16)
            sp.wait_ge(s_const, 1)
            for i, a in enumerate((key_d, src_d)):
                sp.dma_start(a[E:EWINDOWS * CAP].rearrange("(p c) -> p c", p=PADROWS), padt[i]).then_inc(edges_out, 16)
            sp.dma_start(root_sb[:, :, :], root0.rearrange("(k p) e -> p k e", p=P)).then_inc(weights_in, 16)
            for v, a in ((bias_sb[0], bias0), (bias_sb[1], bias1), (gamma_sb, gamma), (beta_sb, beta)):
                with nc.allow_non_contiguous_dma(reason="256 values once"):
                    sp.dma_start(v, a.rearrange("(k p) -> p k", p=P)).then_inc(weights_in, 16)
            for v, a in zip(comp_sb, (comp0, comp1)):
                sp.dma_start(v, a.rearrange("r b -> (r b)").partition_broadcast(P)).then_inc(weights_in, 16)
            with nc.allow_non_contiguous_dma(reason="4096 values once"):
                sp.dma_start(b1_sb.rearrange("p (e c) -> p e c", e=EXPERTS),
                             b1.rearrange("e (c p) -> p e c", p=P)).then_inc(weights_in, 16)
            sp.dma_start(linb_sb[:, :], lin_b).then_inc(weights_in, 16)
            sp.dma_start(b2_sb[:, :], b2).then_inc(weights_in, 16)
            sp.dma_start(br_sb[:, :], br.rearrange("(a e) -> a e", a=1)).then_inc(weights_in, 16)
            sp.dma_start(wr_sb[:, :, :], Wr.rearrange("(k p) e -> p k e", p=P)).then_inc(weights_in, 16)

            sp.wait_ge(edges_out, 64)
            sp.dma_start(basis_sb[:, :, :, :].rearrange("p b k e -> p (b k) e"),
                         basis0.rearrange("b (k p) e -> p (b k) e", p=P)).then_inc(basis_in[0], 16)

            def store_group(i, g):
                sp.wait_ge(g_hi, g + 1)
                sp.wait_ge(g_mid, g + 1)
                sp.wait_ge(g_lo, g + 1)
                dst_ap = tab_g[g] if isinstance(g, int) else tab_g[bass.ds(g, 1), :, :, :].rearrange(
                    "a p t d -> (a p) t d")
                sp.dma_start(dst_ap, gparts[i].rearrange("p t q d -> p t (q d)")).then_inc(g_out[i], 16)

            sp.wait_ge(tables_ready, 1)
            sp.dma_start(idx_d, idx_all[:, :, :]).then_inc(tables_out, 16)
            sp.dma_start(rel_d, rel_all).then_inc(tables_out, 16)

            with sp.Fori(0, (GROUPS - 1) // 2 - 1) as g2:
                for i in range(2):
                    load_group(i, g2 * 2 + i + 2)
                    store_group(i, g2 * 2 + i)
            load_group(0, GROUPS - 1)
            store_group(0, GROUPS - 3)
            store_group(1, GROUPS - 2)
            store_group(0, GROUPS - 1)
            sp.wait_ge(tables_out, 32)

            general = is_general(sp)

            def plain():
                sp.sem_inc(sp_waited, 1)

            def load_edges(h, G, p):
                summed(sp, G, h, back=2)
                plain()
                b = p * 2 + h
                with sp.If(general):
                    sp.dma_start(sums_sb[h], sums_d[bass.ds(b * SLOTS, SLOTS), :].rearrange(
                        "(q p) c -> p q c", p=P)).then_inc(sums_in[h], 16)
                with sp.Else():
                    load_tables(h, b)

            def general_sums(layer):
                sp.wait_ge(zeros_made, layer + 1)
                with sp.Fori(layer * (BLOCKS + 1), (layer + 1) * (BLOCKS + 1)) as b:
                    at = b - layer * (BLOCKS + 1)
                    sp.dma_start(sums_d[bass.ds(at * SLOTS, SLOTS), :].rearrange("(p q) c -> p (q c)", p=P),
                                 zeros).then_inc(sums_cleared, 16)
                    sp.wait_ge(sums_cleared, b * 16 + 16)
                    plain()
                with sp.Fori(0, STEPS) as i:
                    for v, a in ((g_key, key_d), (g_srcf, src_d)):
                        sp.dma_start(v, a[bass.ds(i * P, P)].rearrange("(p a) -> p a", a=1)).then_inc(edge_in, 16)
                    sp.wait_ge(added, i * 16 + (layer * STEPS * 16 + 16))
                    plain()

            def load_tables(h, b):
                cut = bass.ds(b, 1)
                sp.dma_start(idx[:, h, :], idx_d[:, cut, :].rearrange("p a t -> p (a t)")).then_inc(idx_in[h], 16)
                sp.dma_start(rel[:, h, :], rel_d[:, cut, :].rearrange("p a t -> p (a t)")).then_inc(idx_in[h], 16)

            def store_inv(p):
                sp.wait_ge(sc_ready, p * 2 + 2)
                sp.dma_start(inv_p[bass.ds(p, 1), :, :], inv[0:1, :, :]).then_inc(inv_out, 16)

            with sp.If(general):
                for i in range(2):
                    sp.wait_ge(g_out[i], 16 * (4 - i))
                general_sums(0)
            for h in range(2):
                load_edges(h, 0, 0)
            for i in range(2):
                sp.wait_ge(g_out[i], 16 * (4 - i))
            sp.wait_ge(g_Tc, GROUPS)
            sp.dma_start(linw_sb[:, :, :, :].rearrange("p t k d -> p (t k) d"),
                         lin_w.rearrange("t (k p) d -> p (t k) d", p=P)).then_inc(ffn_in, 16)

            def load_expert(e):
                at = bass.ds(e, 1)
                sp.dma_start(w1_sb[:, at, :, :].rearrange("p e k h -> p (e k) h"),
                             W1[at, :, :].rearrange("e (k p) h -> p (e k) h", p=P)).then_inc(ffn_in, 16)
                sp.dma_start(w2_sb[:, at, :, :].rearrange("p e c d -> p (e c) d"),
                             W2[at, :, :].rearrange("e (c p) d -> p (e c) d", p=P)).then_inc(ffn_in, 16)

            def first_layer(p):
                for h in range(2):
                    load_edges(h, p, p)
                store_inv(p - 1)

            with sp.Fori(1, EXPERTS + 1) as p:
                first_layer(p)
                load_expert(p - 1)
            with sp.Fori(EXPERTS + 1, PAIRS) as p:
                first_layer(p)
            store_inv(PAIRS - 1)

            sp.wait_ge(tr_done, PAIRS)
            sp.dma_start(root_sb[:, :, :], root1.rearrange("(k p) e -> p k e", p=P)).then_inc(basis_in[1], 16)
            sp.dma_start(basis_sb[:, :, :, :].rearrange("p b k e -> p (b k) e"),
                         basis1.rearrange("b (k p) e -> p (b k) e", p=P)).then_inc(basis_in[1], 16)
            sp.wait_ge(inv_out, 16 * PAIRS)

            def load_inv(h, G, p):
                sp.wait_ge(sc_ready, (G * 2 + h) - 1)
                sp.dma_start(inv[:, h, :], inv_p[bass.ds(p, 1), h, :].rearrange(
                    "a s -> (a s)").partition_broadcast(P)).then_inc(inv_in[h], 16)

            def load_nodes(p, n=P):
                sp.wait_ge(lin_acc, START + 6 * p)
                at = bass.ds(p * P, n)
                sp.dma_start(xcur[0:n, :], x[at, :]).then_inc(node_in, 16)
                sp.dma_start(ntcol[0:n, :], ntype[at].rearrange("(p a) -> p a", a=1)).then_inc(node_in, 16)
                sp.dma_start(ntrow[:, 0:n], ntype[at].partition_broadcast(TYPES)).then_inc(node_in, 16)

            with sp.If(general):
                sp.wait_ge(parts_out, 16 * PAIRS)
                general_sums(1)
            for h in range(2):
                load_edges(h, PAIRS, 0)
                load_inv(h, PAIRS, 0)
            with sp.Fori(1, PAIRS) as p:
                for h in range(2):
                    load_edges(h, p + PAIRS, p)
                    load_inv(h, p + PAIRS, p)
                load_nodes(p - 1)
            load_nodes(PAIRS - 1, LAST)
            sp.wait_ge(out_done, 16 * PAIRS)

        @block.gpsimd
        def _(gp):
            def plain():
                gp.sem_inc(pool_waited, 1)

            gp.memset(padt[0], PADKEY)
            gp.memset(padt[1], 0.0).then_inc(s_const, 1)
            gp.memset(ones_f[:, :], 1.0)
            gp.memset(ones_b[:, :], 1.0)
            gp.memset(eps_col[:, :], EPS)
            gp.iota(limit_col[:, :], [[0, 1]], base=0, channel_multiplier=SLOTS,
                    allow_small_or_imprecise_dtypes=True)
            gp.iota(limit_row[:, :], [[SLOTS, BLOCKS]], base=0, channel_multiplier=0,
                    allow_small_or_imprecise_dtypes=True)
            gp.iota(iota_b[:, :], [[1, HOT_MAX]], base=0, channel_multiplier=0,
                    allow_small_or_imprecise_dtypes=True)
            gp.iota(iota8[:, :], [[1, EXPERTS]], base=0, channel_multiplier=0,
                    allow_small_or_imprecise_dtypes=True)
            gp.iota(pid[:, :], [[0, 1]], base=0, channel_multiplier=1, allow_small_or_imprecise_dtypes=True)
            gp.memset(ident[:, :], 0.0).then_inc(s_const, 1)
            gp.wait_ge(s_const, 2)
            gp.affine_select(out=ident[:, :], in_=ident[:, :], compare_op=ALU.not_equal, fill=1.0, base=0,
                             pattern=[[-1, P]], channel_multiplier=1).then_inc(s_const, 1)

            gp.wait_ge(row_ready, 1)
            gp.wait_ge(edges_out, 64)
            gp.indirect_dma_start(out=rows, out_offset=None, in_=key_d[0:E].rearrange("(p c) -> p c", c=ECOLS),
                                  in_offset=bass.IndirectOffsetOnAxis(ap=row_i[0:BLOCKS, 0:1], axis=0)).then_inc(rows_in, 16)
            gp.wait_ge(start_ready, 1)
            for i, a in enumerate((key_d, src_d)):
                gp.indirect_dma_start(out=win[:, i, :], out_offset=None,
                                      in_=a.rearrange("(p c) -> p c", c=CAP),
                                      in_offset=bass.IndirectOffsetOnAxis(ap=start_i[0:BLOCKS, 0:1], axis=1)).then_inc(win_in, 16)

            def gather(layer, h, k):
                gp.indirect_dma_start(out=slot[:, k, :], out_offset=None, in_=table[layer],
                                      in_offset=bass.IndirectOffsetOnAxis(ap=idx[:, h, k:k + 1], axis=0)).then_inc(gathered[k], 16)

            def gathers(layer, G):
                blocks = [gp.snap(G * 2 + (START + h)) for h in range(2)]
                for h in range(2):
                    n = blocks[h]
                    gp.wait_ge(idx_in[h], G * 32 + 32)
                    for k in range(TILES):
                        if k % RUN == 0:
                            gp.wait_ge(used[k + RUN - 1], n)
                            plain()
                        if k < TILES - 1:
                            gather(layer, h, k)
                    with gp.If(gp.value_load(last_tile[0:1, bass.ds((G - layer * PAIRS) * 2 + h, 1)], min_val=0,
                                             max_val=1)):
                        gather(layer, h, TILES - 1)

            def general_sums(layer):
                gp.memset(zeros, 0.0)
                gp.memset(below, 0.0).then_inc(zeros_made, 1)
                gp.wait_ge(zeros_made, layer + 1)
                gp.iota(spare_row, [[0, 1]], base=SPARE, channel_multiplier=1,
                        allow_small_or_imprecise_dtypes=True)
                gp.affine_select(out=below, in_=below, compare_op=ALU.is_ge, fill=1.0, base=0,
                                 pattern=[[1, P]], channel_multiplier=-1).then_inc(below_made, 1)
                with gp.Fori(0, STEPS) as i:
                    n = i + layer * STEPS
                    gp.wait_ge(edge_idx, n + 1)
                    plain()
                    gp.indirect_dma_start(out=g_rows, out_offset=None, in_=table[layer],
                                          in_offset=bass.IndirectOffsetOnAxis(ap=g_src, axis=0)).then_inc(edge_rows, 16)
                    gp.wait_ge(dest_ready, n + 1)
                    plain()
                    gp.wait_ge(edge_sum_out, n + 1)
                    plain()
                    gp.indirect_dma_start(out=sums_d, out_offset=bass.IndirectOffsetOnAxis(ap=g_dest, axis=0),
                                          in_=g_sum, in_offset=None, compute_op=ALU.add).then_inc(added, 16)
                    gp.wait_ge(added, n * 16 + 16)
                    plain()

            for i in range(2):
                gp.wait_ge(g_out[i], 16 * (4 - i))
            general = is_general(gp)
            with gp.If(general):
                general_sums(0)
                gp.wait_ge(parts_out, 16 * PAIRS)
                general_sums(1)
            with gp.Else():
                with gp.Fori(0, PAIRS) as p:
                    gathers(0, p)
                gp.wait_ge(parts_out, 16 * PAIRS)
                with gp.Fori(PAIRS, 2 * PAIRS) as p:
                    gathers(1, p)

        @block.scalar
        def _(act_):
            sc = nc.scalar

            def norm_group(i, g):
                act_.wait_ge(g_var, g + 1)
                sc.activation(gvar[:, :], gvar[:, :], ACT.Sqrt, bias=eps_col[:, :]).then_inc(g_std, 1)
                act_.wait_ge(g_stat, g + 1)
                if not isinstance(g, int) or g >= 2:
                    act_.wait_ge(g_Tc, g - 1)
                    act_.wait_ge(g_rest, g - 1)
                for t in range(GROUP):
                    last = sc.activation(xn[i][:, t, :], xg[i][:, t, :], ACT.Identity,
                                         bias=gshift[:, i, t:t + 1], scale=grstd[:, i, t:t + 1])
                last.then_inc(g_norm, 1)
                act_.wait_ge(g_norm, g + 1)
                if not isinstance(g, int) or g >= 2:
                    act_.wait_ge(g_out[i], 8 * (g - i))
                sc.activation(gparts[i][:, :, 0, :], xn[i], ACT.Copy).then_inc(g_hi, 1)
                for j in range(4):
                    n = min(4, 2 * GROUP - 4 * j) // 2
                    act_.wait_ge(g_T, g * 4 + j + 1)
                    node = g * (GROUP * P) + j * 2 * P
                    for k in range(HALVES):
                        last = sc.activation(featT[:, k, bass.ds(node, n * P)],
                                             bank[j][:, k * n * P:(k + 1) * n * P], ACT.Copy)
                last.then_inc(g_Tc, 1)

            norm_group(0, 0)
            norm_group(1, 1)
            with act_.Fori(1, (GROUPS - 1) // 2) as g2:
                for i in range(2):
                    norm_group(i, g2 * 2 + i)
            norm_group(0, GROUPS - 1)

            act_.wait_ge(weights_in, 16 * N_WEIGHTS)

            def relu(layer, G, p):
                act_.wait_ge(tr_done, G + 1)
                if layer == 0:
                    act_.wait_ge(hT_done, p)
                    act_.wait_ge(feat_saved, p)
                for k in range(HALVES):
                    last = sc.activation(hcur[:, k, :], T[:, k * P:(k + 1) * P], ACT.Relu,
                                         bias=bias_sb[layer][:, k:k + 1])
                last.then_inc(relu_done, 1)

            def publish(p):
                act_.wait_ge(hT_done, p + 1)
                act_.wait_ge(parts_out, p * 16)
                sc.activation(parts[:, 0, :], T2[:, 0:D], ACT.Copy).then_inc(hi_done, 1)
                act_.wait_ge(rest_done, START + p + 1)
                sc.activation(parts[:, 1, :], rest[:, :], ACT.Copy).then_inc(mid_done, 1)
                act_.wait_ge(lo_done, START + p + 1)
                act_.wait_ge(mid_done, START + p + 1)
                act_.dma_start(tab_p[bass.ds(p, 1), :, :].rearrange("a p d -> (a p) d"),
                               parts[:, :, :].rearrange("p q d -> p (q d)")).then_inc(parts_out, 16)

            relu(0, 0, 0)
            publish(0)
            with act_.Fori(1, PAIRS) as p:
                relu(0, p, p)
                publish(p)

            def dense(p, n=P):
                act_.wait_ge(out_done, p * 16)
                relu(1, p + PAIRS, p)
                for i in range(2):
                    act_.wait_ge(ln_var, p * 2 + i + 1)
                    sc.activation(std[:, :], mv[:, 1:2], ACT.Sqrt, bias=eps_col[:, :]).then_inc(ln_std, 1)
                act_.wait_ge(znT_done, START + p + 1)
                for k in range(HALVES):
                    last = sc.activation(xnT[:, k, :], T2[:, k * P:(k + 1) * P], ACT.Identity,
                                         bias=beta_sb[:, k:k + 1], scale=gamma_sb[:, k:k + 1])
                last.then_inc(xnT_done, 1)
                for e in range(EXPERTS):
                    act_.wait_ge(h_ps, p * EXPERTS + e + 1)
                    if e >= 2:
                        act_.wait_ge(y_ps, p * EXPERTS + e - 1)
                    for c in range(HCH):
                        last = sc.activation(act[:, e % 2, c, :], HP[e % 2][:, c * P:(c + 1) * P], ACT.Gelu,
                                             bias=b1_sb[:, e * HCH + c:e * HCH + c + 1])
                    last.then_inc(h_act, 1)
                    if e == 0:
                        act_.wait_ge(margin_done, p + 1)
                        sc.activation(soft[:, 1:2], soft[:, 0:1], ACT.Tanh, scale=0.5).then_inc(tanh_done, 1)
                    if e == 3:
                        act_.wait_ge(wfT_ps, p + 1)
                        sc.activation(wfT[:, :], T2[0:EXPERTS, 256:256 + P], ACT.Copy).then_inc(wfT_done, 1)
                act_.wait_ge(y_acc, (p + 1) * EXPERTS)
                act_.dma_start(out[bass.ds(p * P, n), :], o[0:n, :]).then_inc(out_done, 16)

            dense(0)
            with act_.Fori(1, PAIRS - 1) as p:
                dense(p)
            dense(PAIRS - 1, LAST)
            act_.wait_ge(out_done, 16 * PAIRS)

        @block.vector
        def _(dve):
            v = nc.vector
            ch = Chain(dve, s_dve)
            chg = Chain(dve, s_general)

            def plain():
                v.memset(idle[:, :], 0.0)

            dve.wait_ge(s_const, 3)
            for i in range(3):
                dve.wait_ge(raw_in[i], 16)
            v.scalar_tensor_tensor(out=edge_f[0], in0=raw[:, 0, :], scalar=float(R), in1=raw[:, 1, :],
                                   op0=ALU.mult, op1=ALU.add).then_inc(edges_f, 1)
            v.tensor_copy(edge_f[1], raw[:, 2, :]).then_inc(edges_f, 1)
            dve.wait_ge(edges_f, 2)
            v.tensor_scalar(before[0:EROWS, :], limit_row[0:EROWS, :], edge_f[0][:, 0:1], None,
                            ALU.is_gt).then_inc(s_before, 1)
            dve.wait_ge(s_count, 1)
            B = slice(0, BLOCKS)
            ch.link(v.tensor_scalar(found[B, 0:1], T[B, 0:1], -1.0, 0.0, ALU.add, ALU.max))
            v.tensor_copy(row_i[B, :], found[B, 0:1]).then_inc(row_ready, 1)
            def group_stats(i, g):
                dve.wait_ge(xg_in[i], 8 * (g - i) + 16 + (16 if isinstance(g, int) and g == GROUPS - 1 else 0))
                if not isinstance(g, int) or g >= 1:
                    dve.wait_ge(g_norm, g)
                plain()
                for t in range(GROUP):
                    last = v.bn_stats(gstats[:, t, :], xg[i][:, t, :])
                ch.link(last)
                plain()
                for t in range(GROUP):
                    last = v.bn_aggr(gmv[:, t, :], gstats[:, t, :])
                ch.link(last)
                v.tensor_copy(gvar[:, :], gmv[:, :, 1]).then_inc(g_var, 1)
                dve.wait_ge(g_std, g + 1)
                ch.link(v.reciprocal(grstd[:, i, :], gvar[:, :]))
                v.scalar_tensor_tensor(out=gshift[:, i, :], in0=gmv[:, :, 0], scalar=-1.0,
                                       in1=grstd[:, i, :], op0=ALU.mult, op1=ALU.mult).then_inc(g_stat, 1)

            def group_parts(i, g):
                dve.wait_ge(g_hi, g + 1)
                if not isinstance(g, int) or g >= 1:
                    dve.wait_ge(g_lo, g)
                v.tensor_tensor(grest, xn[i], gparts[i][:, :, 0, :], ALU.subtract).then_inc(g_rest, 1)
                dve.wait_ge(g_rest, g + 1)
                v.tensor_copy(gparts[i][:, :, 1, :], grest).then_inc(g_mid, 1)
                dve.wait_ge(g_mid, g + 1)
                v.tensor_tensor(gparts[i][:, :, 2, :], grest, gparts[i][:, :, 1, :],
                                ALU.subtract).then_inc(g_lo, 1)

            GL = 3
            group_stats(0, 0)
            dve.wait_ge(rows_in, 16)
            ch.link(v.tensor_scalar(rows, rows, limit_col[B, 0:1], None, ALU.is_lt))
            ch.link(v.tensor_reduce(found[B, 1:2], rows, AX.X, ALU.add))
            ch.link(v.scalar_tensor_tensor(out=found[B, 2:3], in0=found[B, 0:1], scalar=float(ECOLS),
                                           in1=found[B, 1:2], op0=ALU.mult, op1=ALU.add))
            v.tensor_copy(start_i[B, :], found[B, 2:3]).then_inc(start_ready, 1)

            group_stats(1, 1)
            dve.wait_ge(win_in, 32)
            v.tensor_scalar(win[:, 0, :], win[:, 0, :], limit_col[B, 0:1], None,
                            ALU.subtract).then_inc(win_rel, 1)
            for j in range(TILES // 2):
                dve.wait_ge(win_T, j + 1)
                for a in range(2):
                    k = 2 * j + a
                    pb = bank[4 + j % 2][:, a * 256:a * 256 + BLOCKS]
                    pi = bank[4 + j % 2][:, a * 256 + P:a * 256 + P + BLOCKS]
                    v.tensor_scalar(rel_all[:, :, k], pb, float(-R * WIN[k][0]), None, ALU.add)
                    last = v.tensor_copy(idx_all[:, :, k], pi)
                last.then_inc(win_copied, 1)
            dve.wait_ge(win_copied, TILES // 2)
            ch.link(v.tensor_scalar(in_window, rel_all, 0.0, None, ALU.is_ge))
            for k in range(TILES):
                last = v.scalar_tensor_tensor(out=in_window[:, :, k], in0=rel_all[:, :, k],
                                              scalar=float(HOT_AT[k + 1] - HOT_AT[k]), in1=in_window[:, :, k],
                                              op0=ALU.is_lt, op1=ALU.mult)
            ch.link(last)
            v.tensor_copy(in_last[:, :], in_window[:, :, TILES - 1])
            v.tensor_reduce(found[:, 3:4], in_window, AX.XY, ALU.add).then_inc(matched, 1)
            dve.wait_ge(matched_sum, 1)
            ch.link(v.tensor_scalar(found[B, 0:1], limit_col[B, :], 1.0, None, ALU.min))
            v.tensor_scalar(found[B, 1:2], C[B, 1:2], found[B, 0:1], None, ALU.is_ge)
            v.tensor_scalar(up_to[B, :], limit_row[B, :], limit_col[B, 0:1], None,
                            ALU.is_ge).then_inc(last_known, 1)
            dve.wait_ge(last_summed, 1)
            v.tensor_copy(last_tile[:, :], C[0:1, P:P + BLOCKS])
            ch.link(v.tensor_scalar(last_count[:, 0, :], C[0:1, 2 * P:2 * P + BLOCKS], 16.0, None, ALU.mult))
            v.tensor_scalar(last_count[:, 1, :], C[0:1, 2 * P:2 * P + BLOCKS],
                            C[0:1, 2 * P + BLOCKS - 1:2 * P + BLOCKS], 16.0, ALU.add, ALU.mult)
            v.tensor_scalar(general_i[:, :], C[0:1, 0:1], float(E), None, ALU.is_lt).then_inc(general_known, 1)
            v.memset(idle[:, :], 0.0).then_inc(tables_ready, 1)

            group_parts(0, 0)
            ch0 = ch.n - 2 * GL
            with dve.Fori(1, (GROUPS - 1) // 2) as g2:
                for i in range(2):
                    ch.begin(g2 * (2 * GL) + (ch0 + i * GL))
                    group_stats(i, g2 * 2 + i)
                    group_parts(1 - i, g2 * 2 + i - 1)
            ch.begin(ch0 + GL * (GROUPS - 1))
            group_stats(0, GROUPS - 1)
            group_parts(1, GROUPS - 2)
            group_parts(0, GROUPS - 1)

            general = is_general(dve)

            def general_sums(layer):
                dve.wait_ge(below_made, layer + 1)
                with dve.Fori(0, STEPS) as i:
                    n = i + layer * STEPS
                    chg.begin(n * 3)
                    dve.wait_ge(edge_in, n * 32 + 32)
                    v.tensor_copy(g_src, g_srcf).then_inc(edge_idx, 1)
                    dve.wait_ge(key_row, n + 1)
                    chg.link(v.tensor_scalar(same, T[:, 0:P], g_key, None, ALU.is_equal))
                    chg.link(v.tensor_tensor(before_me, same, below, ALU.mult))
                    v.tensor_reduce(g_tmp[:, 0:1], before_me, AX.X, ALU.add).then_inc(same_ready, 1)
                    dve.wait_ge(same_ready, n + 1)
                    v.tensor_scalar(g_tmp[:, 1:2], g_tmp[:, 0:1], 0.5, None, ALU.is_lt)
                    chg.link(v.tensor_tensor(g_tmp[:, 2:3], g_key, spare_row, ALU.subtract))
                    v.scalar_tensor_tensor(out=g_dest, in0=g_tmp[:, 2:3], scalar=g_tmp[:, 1:2], in1=spare_row,
                                           op0=ALU.mult, op1=ALU.add).then_inc(dest_ready, 1)
                    dve.wait_ge(edge_sum, n + 1)
                    v.tensor_copy(g_sum, T2[:, 0:MCOLS]).then_inc(edge_sum_out, 1)
                    assert chg.n == 3

            def mix_bases(layer, G, nodes, first=0, last_=MIXES):
                if first == 0:
                    if not isinstance(G, int) or G > 0:
                        dve.wait_ge(tr_done, G)
                    dve.wait_ge(sc_ready, G * 2 + nodes.stop // BD)
                for j in range(first, last_):
                    r, b = divmod(j, NBASIS)
                    s = comp_sb[layer][:, r * NBASIS + b:r * NBASIS + b + 1]
                    if r == 0:
                        ins = v.tensor_scalar(mixed[:, b, :, nodes], scaled[:, :, r, nodes], s, None, ALU.mult)
                    else:
                        ins = v.scalar_tensor_tensor(out=mixed[:, b, :, nodes], in0=scaled[:, :, r, nodes],
                                                     scalar=s, in1=mixed[:, b, :, nodes], op0=ALU.mult, op1=ALU.add)
                    if b == NBASIS - 1 and r < R - 1:
                        ch.link(ins)
                if last_ == MIXES and nodes.stop == P:
                    ins.then_inc(mixed_ready, 1)

            def one_hots(h, G):
                with dve.If(general):
                    pass
                with dve.Else():
                    one_hots_fast(h, G)

            def one_hots_fast(h, G):
                dve.wait_ge(idx_in[h], G * 32 + 32)
                summed(dve, G, h, back=2)
                for k in range(TILES):
                    w = HOT_AT[k + 1] - HOT_AT[k]
                    last = v.tensor_scalar(hot[:, h, HOT_AT[k]:HOT_AT[k + 1]], iota_b[:, 0:w],
                                           rel[:, h, k:k + 1], None, ALU.is_equal)
                last.then_inc(hot_ready, 1)

            def scale(layer, h, G, p):
                summed(dve, G, h)
                iv = inv[:, h, :]
                if layer == 0:
                    dve.wait_ge(inv_out, p * 16)
                    ch.link(v.tensor_scalar(iv, C[:, :], 1.0, None, ALU.max))
                    ch.link(v.reciprocal(iv, iv))
                else:
                    dve.wait_ge(inv_in[h], p * 16 + 16)
                if h == 0:
                    dve.wait_ge(mixed_ready, G)
                for k in range(HALVES):
                    last = v.tensor_tensor(
                        scaled[:, k, :, h * BD:(h + 1) * BD].rearrange("p r n -> p n r"),
                        S[k][:, :].rearrange("p (n r) -> p n r", r=R),
                        iv.rearrange("p (n r) -> p n r", r=R), ALU.mult)
                last.then_inc(sc_ready, 1)

            def save(p):
                dve.wait_ge(relu_done, START + p + 1)
                v.tensor_copy(featT[:, :, bass.ds(p * P, P)], hcur[:, :, :]).then_inc(feat_saved, 1)
                dve.wait_ge(hi_done, p + 1)
                dve.wait_ge(mid_done, START + p)
                dve.wait_ge(lo_done, START + p)
                v.tensor_tensor(rest[:, :], T2[:, 0:D], parts[:, 0, :], ALU.subtract).then_inc(rest_done, 1)
                dve.wait_ge(mid_done, START + p + 1)
                v.tensor_tensor(parts[:, 2, :], rest[:, :], parts[:, 1, :], ALU.subtract).then_inc(lo_done, 1)

            def layer_norm(dst_, src_, count):
                plain()
                ch.link(v.bn_stats(stats[:, :], src_))
                plain()
                v.bn_aggr(mv[:, :], stats[:, :]).then_inc(ln_var, 1)
                dve.wait_ge(ln_std, count)
                ch.link(v.reciprocal(rstd[:, :], std[:, :]))
                return v.tensor_scalar(dst_, src_, mv[:, 0:1], rstd[:, 0:1], ALU.subtract, ALU.mult)

            def masks(p):
                dve.wait_ge(node_in, p * 48 + 48)
                v.tensor_scalar(tmask[:, :], iota8[:, 0:TYPES], ntcol[:, 0:1], None, ALU.is_equal)
                v.tensor_scalar(tmaskT[:, :], ntrow[:, :], pid[0:TYPES, 0:1], None,
                                ALU.is_equal).then_inc(mask_done, 1)
                dve.wait_ge(mask_done, p + 1)

            def typed(p):
                if not isinstance(p, int) or p > 0:
                    dve.wait_ge(y_acc, p * EXPERTS)
                for j in range(TYPES + 1):
                    dve.wait_ge(lin_ps, p * 6 + j + 1)
                    acc = xcur if j == 0 else x1
                    s = tmask[:, j:j + 1] if j < TYPES else 1.0
                    v.scalar_tensor_tensor(out=x1[:, :], in0=YP[j % 2][:, 0:D], scalar=s, in1=acc[:, :],
                                           op0=ALU.mult, op1=ALU.add).then_inc(lin_acc, 1)
                    dve.wait_ge(lin_acc, START + p * 6 + j + 1)
                dve.wait_ge(znT_done, START + p)
                ch.link(layer_norm(zn[:, :], x1[:, :], p * 2 + 1))
                layer_norm(zn[:, :], zn[:, :], p * 2 + 2).then_inc(zn_done, 1)

            def route(p):
                dve.wait_ge(lg_done, p + 1)
                v.tensor_copy(lg[:, :], T[:, 0:EXPERTS]).then_inc(lg_read, 1)
                dve.wait_ge(lg_read, p + 1)
                plain()
                ch.link(v.max(top[:, :], lg[:, :]))
                plain()
                ch.link(v.max_index(topi[:, :], top[:, :], lg[:, :]))
                v.tensor_copy(topf[:, :], topi[:, 0:2])
                v.tensor_tensor(soft[:, 0:1], top[:, 0:1], top[:, 1:2], ALU.subtract).then_inc(margin_done, 1)
                dve.wait_ge(tanh_done, p + 1)
                v.tensor_scalar(soft[:, 2:3], soft[:, 1:2], 0.5, 0.5, ALU.mult, ALU.add)
                ch.link(v.tensor_scalar(soft[:, 3:4], soft[:, 1:2], -0.5, 0.5, ALU.mult, ALU.add))
                v.tensor_scalar(wfull[:, 0, :], iota8[:, :], topf[:, 0:1], soft[:, 2:3], ALU.is_equal, ALU.mult)
                ch.link(v.tensor_scalar(wfull[:, 1, :], iota8[:, :], topf[:, 1:2], soft[:, 3:4],
                                        ALU.is_equal, ALU.mult))
                v.tensor_tensor(wfull[:, 0, :], wfull[:, 0, :], wfull[:, 1, :], ALU.add).then_inc(wf_done, 1)
                dve.wait_ge(wf_done, p + 1)

            def mix(p, between=lambda e: None):
                for e in range(EXPERTS):
                    dve.wait_ge(y_ps, p * EXPERTS + e + 1)
                    acc = x1 if e == 0 else o
                    v.scalar_tensor_tensor(out=o[:, :], in0=YP[e % 2][:, 0:D], scalar=wfull[:, 0, e:e + 1],
                                           in1=acc[:, :], op0=ALU.mult, op1=ALU.add).then_inc(y_acc, 1)
                    if e < EXPERTS - 1:
                        dve.wait_ge(y_acc, p * EXPERTS + e + 1)
                    if e == 5:
                        dve.wait_ge(b2_ps, p + 1)
                        v.tensor_tensor(o[:, :], o[:, :], T[:, 0:D], ALU.add).then_inc(b2_added, 1)
                        dve.wait_ge(b2_added, START + p + 1)
                    between(e)

            def layer_steps(layer):
                g0 = layer * PAIRS
                one_hots(0, g0)
                one_hots(1, g0)
                for h in range(2):
                    scale(layer, h, g0, 0)
                    mix_bases(layer, g0, slice(h * BD, (h + 1) * BD))
                    one_hots(h, g0 + 1)
                base = ch.base + ch.n

                def body(p, more=True):
                    G = p + g0

                    if layer == 0:
                        scale(layer, 0, G, p)
                        if more:
                            one_hots(0, G + 1)
                        mix_bases(layer, G, slice(0, BD))
                        scale(layer, 1, G, p)
                        if more:
                            save(p - 1)
                            mix_bases(layer, G, slice(BD, P))
                            one_hots(1, G + 1)
                        else:
                            mix_bases(layer, G, slice(BD, P))
                            save(p - 1)
                        return
                    masks(p - 1)
                    typed(p - 1)
                    scale(layer, 0, G, p)
                    route(p - 1)

                    def between(e):
                        if e == 0 and more:
                            plain()
                            one_hots(0, G + 1)
                        if e in (1, 2):
                            mix_bases(layer, G, slice(0, BD), (e - 1) * MIXES // 2, e * MIXES // 2)
                        if e == 2:
                            scale(layer, 1, G, p)
                        if 3 <= e < 6:
                            mix_bases(layer, G, slice(BD, P), (0, 12, 24)[e - 3], (12, 24, 32)[e - 3])

                    mix(p - 1, between)
                    if more:
                        one_hots(1, G + 1)

                per = (4 if layer == 0 else 5 + 4) + 2 * (R - 1)
                with dve.Fori(1, PAIRS - 1) as p:
                    ch.begin(p * per + (base - per))
                    body(p)
                    assert ch.n == per, ch.n
                ch.begin(base + per * (PAIRS - 2))
                body(PAIRS - 1, more=False)
                if layer == 0:
                    save(PAIRS - 1)
                else:
                    masks(PAIRS - 1)
                    typed(PAIRS - 1)
                    route(PAIRS - 1)
                    mix(PAIRS - 1)

            dve.wait_ge(weights_in, 16 * N_WEIGHTS)
            dve.wait_ge(tables_out, 32)
            with dve.If(general):
                general_sums(0)
            layer_steps(0)
            with dve.If(general):
                general_sums(1)
            layer_steps(1)

        @block.tensor
        def _(pe):
            t = nc.tensor
            pe.wait_ge(s_const, 3)
            pe.wait_ge(s_before, 1)
            t.matmul(T[0:BLOCKS, 0:1], before[0:EROWS, :], ones_f[0:EROWS, 0:1], start=True,
                     stop=True).then_inc(s_count, 1)

            def turn_group(i, g):
                pe.wait_ge(g_norm, g + 1)
                pe.wait_ge(g_Tc, g)
                for j in range(4):
                    n = min(4, 2 * GROUP - 4 * j) // 2
                    for k in range(HALVES):
                        for a in range(n):
                            last = t.transpose(bank[j][:, (k * n + a) * P:(k * n + a + 1) * P],
                                               xn[i][:, 2 * j + a, k * P:(k + 1) * P], ident[:, :])
                    last.then_inc(g_T, 1)

            pe.wait_ge(row_ready, 1)
            turn_group(0, 0)
            turn_group(1, 1)
            pe.wait_ge(win_rel, 1)
            for j in range(TILES // 2):
                if j >= 2:
                    pe.wait_ge(win_copied, j - 1)
                for a in range(2):
                    k = 2 * j + a
                    t.transpose(bank[4 + j % 2][:, a * 256:a * 256 + BLOCKS], win[:, 0, k * P:(k + 1) * P],
                                ident[0:BLOCKS, 0:BLOCKS])
                    last = t.transpose(bank[4 + j % 2][:, a * 256 + P:a * 256 + P + BLOCKS],
                                       win[:, 1, k * P:(k + 1) * P], ident[0:BLOCKS, 0:BLOCKS])
                last.then_inc(win_T, 1)
            pe.wait_ge(win_copied, TILES // 2)

            pe.wait_ge(matched, 1)
            t.matmul(C[0:1, 0:1], ones_f[:, 0:1], found[:, 3:4], start=True, stop=True)
            t.matmul(C[0:BLOCKS, 1:2], in_last[:, :], ones_f[:, 0:1], start=True,
                     stop=True).then_inc(matched_sum, 1)
            pe.wait_ge(last_known, 1)
            has_last = found[0:BLOCKS, 1:2]
            t.matmul(C[0:1, P:P + BLOCKS], has_last, ident[0:BLOCKS, 0:BLOCKS], start=True, stop=True)
            t.matmul(C[0:1, 2 * P:2 * P + BLOCKS], has_last, up_to[0:BLOCKS, :], start=True,
                     stop=True).then_inc(last_summed, 1)
            with pe.Fori(1, (GROUPS - 1) // 2) as g2:
                for i in range(2):
                    turn_group(i, g2 * 2 + i)
            turn_group(0, GROUPS - 1)

            general = is_general(pe)

            def general_sums(layer):
                with pe.Fori(0, STEPS) as i:
                    n = i + layer * STEPS
                    pe.wait_ge(edge_in, n * 32 + 32)
                    t.matmul(T[:, 0:P], g_key.broadcast_to([P, P]), ident[:, :], start=True,
                             stop=True).then_inc(key_row, 1)
                    pe.wait_ge(same_ready, n + 1)
                    pe.wait_ge(edge_rows, n * 16 + 16)
                    t.matmul(T2[:, D:MCOLS], same, ones_b[:, 0:1], start=True, stop=True)
                    for q in range(PARTS):
                        last = t.matmul(T2[:, 0:D], same, g_rows[:, q * D:(q + 1) * D], start=(q == 0),
                                        stop=(q == PARTS - 1))
                    last.then_inc(edge_sum, 1)

            def aggregate(layer, h, G, late=()):
                pe.wait_ge(sc_ready, G * 2 + h)
                with pe.If(general):
                    pe.wait_ge(sums_in[h], G * 16 + 16)
                    for q in range(QUADS):
                        at = slice(q * P, (q + 1) * P)
                        if layer == 0:
                            t.matmul(C[:, at], sums_sb[h][:, q, D:MCOLS].broadcast_to([P, P]), ident[:, :],
                                     start=True, stop=True)
                        for f in range(HALVES):
                            last = t.transpose(S[f][:, at], sums_sb[h][:, q, f * P:(f + 1) * P], ident[:, :])
                    last.then_inc(used[TILES - 1], 1)
                    for _, step in late:
                        step()
                with pe.Else():
                    aggregate_fast(layer, h, G, late)

            def aggregate_fast(layer, h, G, late):
                pe.wait_ge(hot_ready, G * 2 + h + 1)
                full = pe.snap(G * 32 + (h * 16 + 16)) if not isinstance(G, int) else G * 32 + h * 16 + 16
                at = (G - layer * PAIRS) * 2 + h
                at = slice(at, at + 1) if isinstance(at, int) else bass.ds(at, 1)
                last_full = pe.value_load(last_count[0:1, layer, at], min_val=16, max_val=32 * BLOCKS)
                for k in range(TILES):
                    lo, hi = WIN[k]
                    oh = hot[:, h, HOT_AT[k]:HOT_AT[k + 1]]
                    for at, step in late:
                        if k == at:
                            step()
                    pe.wait_ge(gathered[k], full if k < TILES - 1 else last_full)
                    if layer == 0:
                        t.matmul(C[:, R * lo:R * hi], ones_b[:, :], oh, start=(k == 0), stop=(k == TILES - 1),
                                 skip_group_check=True)
                    for f in range(HALVES):
                        for q in range(PARTS):
                            last = t.matmul(S[f][:, R * lo:R * hi],
                                            slot[:, k, q * D + f * P:q * D + (f + 1) * P], oh,
                                            start=(k == 0 and q == 0), stop=(k == TILES - 1 and q == PARTS - 1),
                                            skip_group_check=True)
                    if k % RUN == RUN - 1:
                        last.then_inc(used[k], 1)

            def transform(layer, G, p):
                pe.wait_ge(mixed_ready, G + 1)
                if layer == 0:
                    pe.wait_ge(relu_done, START + p)
                else:
                    pe.wait_ge(b2_added, START + p)
                for o_ in range(HALVES):
                    n = 0
                    for k in range(HALVES):
                        t.matmul(T[:, o_ * P:(o_ + 1) * P], root_sb[:, k, o_ * P:(o_ + 1) * P],
                                 featT[:, k, bass.ds(p * P, P)], start=(k == 0), stop=False)
                        for b in range(NBASIS):
                            n += 1
                            last = t.matmul(T[:, o_ * P:(o_ + 1) * P], basis_sb[:, b, k, o_ * P:(o_ + 1) * P],
                                            mixed[:, b, k, :], start=False, stop=(n == NBASIS * HALVES))
                last.then_inc(tr_done, 1)

            def turn(p):
                pe.wait_ge(relu_done, START + p + 1)
                pe.wait_ge(rest_done, START + p)
                for k in range(HALVES):
                    last = t.transpose(T2[:, k * P:(k + 1) * P], hcur[:, k, :], ident[:, :])
                last.then_inc(hT_done, 1)

            def typed(p):
                pe.wait_ge(relu_done, START + p + (PAIRS + 1))
                pe.wait_ge(mask_done, p + 1)
                for j in range(TYPES + 1):
                    if j >= 2:
                        pe.wait_ge(lin_acc, START + p * 6 + (j - 1))
                    Y = YP[j % 2][:, 0:D]
                    if j < TYPES:
                        t.matmul(Y, hcur[:, 0, :], linw_sb[:, j, 0, :], start=True, stop=False)
                        last = t.matmul(Y, hcur[:, 1, :], linw_sb[:, j, 1, :], start=False, stop=True)
                    else:
                        last = t.matmul(Y, tmaskT[:, :], linb_sb[:, :], start=True, stop=True)
                    last.then_inc(lin_ps, 1)

            def turn_normed(p):
                pe.wait_ge(zn_done, p + 1)
                for k in range(HALVES):
                    last = t.transpose(T2[:, k * P:(k + 1) * P], zn[:, k * P:(k + 1) * P], ident[:, :])
                last.then_inc(znT_done, 1)

            def experts(p, between=lambda: None):
                pe.wait_ge(xnT_done, p + 1)
                for k in range(HALVES):
                    t.matmul(T[:, 0:EXPERTS], xnT[:, k, :], wr_sb[:, k, :], start=(k == 0), stop=False)
                t.matmul(T[:, 0:EXPERTS], ones_f[0:1, :], br_sb[:, :], start=False, stop=True).then_inc(lg_done, 1)

                def up(e):
                    if e >= 2:
                        pe.wait_ge(h_act, p * EXPERTS + (e - 1))
                    for c in range(HCH):
                        for k in range(HALVES):
                            last = t.matmul(HP[e % 2][:, c * P:(c + 1) * P], w1_sb[:, e, k, c * P:(c + 1) * P],
                                            xnT[:, k, :], start=(k == 0), stop=(k == HALVES - 1))
                    last.then_inc(h_ps, 1)

                def down(e):
                    pe.wait_ge(h_act, p * EXPERTS + (e + 1))
                    if e >= 2:
                        pe.wait_ge(y_acc, p * EXPERTS + (e - 1))
                    else:
                        pe.wait_ge(lin_acc, START + p * 6 + 6)
                    for c in range(HCH):
                        last = t.matmul(YP[e % 2][:, 0:D], act[:, e % 2, c, :], w2_sb[:, e, c, :],
                                        start=(c == 0), stop=(c == HCH - 1))
                    last.then_inc(y_ps, 1)

                up(0)
                up(1)
                for e in range(EXPERTS):
                    down(e)
                    if e + 2 < EXPERTS:
                        up(e + 2)
                    if e == 2:
                        between()
                    if e == 1:
                        pe.wait_ge(wf_done, p + 1)
                        t.transpose(T2[0:EXPERTS, 256:256 + P], wfull[:, 0, :], ident[:, :]).then_inc(wfT_ps, 1)
                    if e == 4:
                        pe.wait_ge(wfT_done, p + 1)
                        t.matmul(T[:, 0:D], wfT[:, :], b2_sb[:, :], start=True, stop=True).then_inc(b2_ps, 1)

            pe.wait_ge(g_Tc, GROUPS)
            pe.wait_ge(weights_in, 16 * N_WEIGHTS)
            with pe.If(general):
                general_sums(0)
            aggregate(0, 0, 0)
            aggregate(0, 1, 0)
            pe.wait_ge(basis_in[0], 16)
            with pe.Fori(1, PAIRS) as p:
                aggregate(0, 0, p)
                transform(0, p - 1, p - 1)
                aggregate(0, 1, p)
                turn(p - 1)
            transform(0, PAIRS - 1, PAIRS - 1)
            turn(PAIRS - 1)
            with pe.If(general):
                general_sums(1)
            aggregate(1, 0, PAIRS)
            aggregate(1, 1, PAIRS)
            pe.wait_ge(basis_in[1], 32)
            pe.wait_ge(ffn_in, 16 * (2 * EXPERTS + 1))
            pe.wait_ge(feat_saved, PAIRS)
            with pe.Fori(1, PAIRS) as p:
                transform(1, p + (PAIRS - 1), p - 1)
                aggregate(1, 0, p + PAIRS, ((RUN + 1, lambda: typed(p - 1)),
                                            (TILES - RUN, lambda: turn_normed(p - 1))))
                experts(p - 1, lambda: aggregate(1, 1, p + PAIRS))
            transform(1, 2 * PAIRS - 1, PAIRS - 1)
            typed(PAIRS - 1)
            turn_normed(PAIRS - 1)
            experts(PAIRS - 1)


_INS = ['x', 'src', 'dst', 'edge_type_8', 'node_type_5', 'L0_gnn_basis0', 'L0_gnn_comp0', 'L0_gnn_root0',
        'L0_gnn_bias0', 'L0_gnn_basis1', 'L0_gnn_comp1', 'L0_gnn_root1', 'L0_gnn_bias1', 'L0_gnn_lin_w',
        'L0_gnn_lin_b', 'L0_ffn_gamma', 'L0_ffn_beta', 'L0_ffn_Wr', 'L0_ffn_br', 'L0_ffn_W1', 'L0_ffn_b1',
        'L0_ffn_W2', 'L0_ffn_b2']


def kernel(**inputs):
    import numpy as _np
    import concourse.bacc as _bacc
    from concourse import mybir as _mybir
    from concourse.bass_utils import run_bass_kernel_spmd as _run

    nc = _bacc.Bacc("TRN2", target_bir_lowering=False, num_devices=1)
    arrays, args = {}, []
    for name in _INS:
        a = _np.ascontiguousarray(inputs[name])
        arrays[f"in_{name}_dram"] = a
        args.append(nc.dram_tensor(f"in_{name}_dram", a.shape, _mybir.dt.from_np(a.dtype), kind="ExternalInput").ap())
    args.append(nc.dram_tensor("out_0_dram", (N, D), _mybir.dt.float32, kind="ExternalOutput").ap())
    build(nc, *args)
    r = _run(nc, [arrays], core_ids=[0])
    return r.results[0]["out_0_dram"]
```
